# Optimizing a Trainium2 kernel written in Bass

```python
import numpy as np
import jax
import jax.numpy as jnp

def _softmax(x, axis=-1):
    return jax.nn.softmax(x, axis=axis)

def _gelu(x):
    return jax.nn.gelu(x, approximate=True)

def _silu(x):
    return jax.nn.silu(x)

def _sigmoid(x):
    return jax.nn.sigmoid(x)

def _layernorm(x, axis=-1, eps=1e-05):
    m = jnp.mean(x, axis=axis, keepdims=True)
    v = jnp.var(x, axis=axis, keepdims=True)
    return (x - m) / jnp.sqrt(v + eps)

def _scatter_add(tgt, idx, src, axis=0):
    return tgt.at[idx].add(src)

def _segment_sum(src, seg, n):
    return jax.ops.segment_sum(src, seg, n)
kernel_name = 'mk_adj_preln_d2_adj_r2_76f7c5'

def setup_inputs(seed: int=0):
    np.random.seed(seed)
    _w = jnp.asarray

    def _rec_inputs():
        import jax
        import jax.numpy as jnp
        _gk = jax.random.key(seed)
        x = -0.0002928 + 1 * jax.random.normal(jax.random.fold_in(_gk, 1), (1354, 256), jnp.float32)
        _a = jax.random.bernoulli(jax.random.fold_in(_gk, 2), 0.00590842, (1354, 1354))
        _a = jnp.logical_or(_a, jnp.swapaxes(_a, -1, -2))
        _a = jnp.logical_or(_a, jnp.eye(1354, dtype=bool))
        adj = _a.astype(jnp.int32)
        return (x, adj)
    x, adj = _rec_inputs()

    def _L0_gnn_setup():
        import jax, jax.numpy as jnp
        import numpy as np
        NEG_BIG = -9000000000000000.0

        def leaky_relu(x, negative_slope=0.01):
            return jnp.where(x >= 0, x, negative_slope * x)
        key = jax.random.key(seed)
        k1, k2, k3 = jax.random.split(key, 3)
        N, dim = (4096, 256)
        x = jax.random.normal(k1, (N, dim), dtype=jnp.float32)
        adj = jax.random.randint(k2, (N, N), 0, 2, dtype=jnp.int32)
        stdv = 1.0 / np.sqrt(dim)
        a = jax.random.uniform(k3, (2 * dim, 1), dtype=jnp.float32, minval=-stdv, maxval=stdv)
        return {'input': x, 'adj_matrix': adj, 'a': a}
    _L0_gnn_all = _L0_gnn_setup()
    _L0_gnn_in = {k: v for k, v in _L0_gnn_all.items() if k in ('a',)}
    del _L0_gnn_all

    def _L1_gnn_setup():
        import jax, jax.numpy as jnp
        import numpy as np
        N = 2048
        STATE_DIM = 256
        OUTPUT_DIM = 256
        N_STEPS = 5
        W_STD = 0.02

        def _lin_params(key, out_dim, in_dim):
            W = jax.random.normal(key, (out_dim, in_dim), dtype=jnp.float32) * W_STD
            b = jnp.zeros((out_dim,), dtype=jnp.float32)
            return (W, b)
        key = jax.random.key(seed)
        ks = jax.random.split(key, 10)
        prop_state = jax.random.normal(ks[0], (N, STATE_DIM), dtype=jnp.float32)
        A = jax.random.randint(ks[1], (N, N), 0, 2, dtype=jnp.int64)
        in_W, in_b = _lin_params(ks[2], STATE_DIM, STATE_DIM)
        out_W, out_b = _lin_params(ks[3], STATE_DIM, STATE_DIM)
        r_W, r_b = _lin_params(ks[4], STATE_DIM, 3 * STATE_DIM)
        z_W, z_b = _lin_params(ks[5], STATE_DIM, 3 * STATE_DIM)
        h_W, h_b = _lin_params(ks[6], STATE_DIM, 3 * STATE_DIM)
        o1_W, o1_b = _lin_params(ks[7], STATE_DIM, STATE_DIM)
        o2_W, o2_b = _lin_params(ks[8], OUTPUT_DIM, STATE_DIM)
        return {'prop_state': prop_state, 'A': A, 'in_W': in_W, 'in_b': in_b, 'out_W': out_W, 'out_b': out_b, 'r_W': r_W, 'r_b': r_b, 'z_W': z_W, 'z_b': z_b, 'h_W': h_W, 'h_b': h_b, 'o1_W': o1_W, 'o1_b': o1_b, 'o2_W': o2_W, 'o2_b': o2_b}
    _L1_gnn_all = _L1_gnn_setup()
    _L1_gnn_in = {k: v for k, v in _L1_gnn_all.items() if k in ('in_W', 'in_b', 'out_W', 'out_b', 'r_W', 'r_b', 'z_W', 'z_b', 'h_W', 'h_b', 'o1_W', 'o1_b', 'o2_W', 'o2_b')}
    del _L1_gnn_all
    return {'x': x, 'adj': adj, 'L0_gnn_a': _L0_gnn_in['a'], 'L1_gnn_in_W': _L1_gnn_in['in_W'], 'L1_gnn_in_b': _L1_gnn_in['in_b'], 'L1_gnn_out_W': _L1_gnn_in['out_W'], 'L1_gnn_out_b': _L1_gnn_in['out_b'], 'L1_gnn_r_W': _L1_gnn_in['r_W'], 'L1_gnn_r_b': _L1_gnn_in['r_b'], 'L1_gnn_z_W': _L1_gnn_in['z_W'], 'L1_gnn_z_b': _L1_gnn_in['z_b'], 'L1_gnn_h_W': _L1_gnn_in['h_W'], 'L1_gnn_h_b': _L1_gnn_in['h_b'], 'L1_gnn_o1_W': _L1_gnn_in['o1_W'], 'L1_gnn_o1_b': _L1_gnn_in['o1_b'], 'L1_gnn_o2_W': _L1_gnn_in['o2_W'], 'L1_gnn_o2_b': _L1_gnn_in['o2_b']}

def reference(x, adj, L0_gnn_a, L1_gnn_in_W, L1_gnn_in_b, L1_gnn_out_W, L1_gnn_out_b, L1_gnn_r_W, L1_gnn_r_b, L1_gnn_z_W, L1_gnn_z_b, L1_gnn_h_W, L1_gnn_h_b, L1_gnn_o1_W, L1_gnn_o1_b, L1_gnn_o2_W, L1_gnn_o2_b):
    import jax
    import jax.numpy as jnp

    def _L0_gnn_ref(input, adj_matrix, a):
        import jax, jax.numpy as jnp
        import numpy as np
        NEG_BIG = -9000000000000000.0

        def leaky_relu(x, negative_slope=0.01):
            return jnp.where(x >= 0, x, negative_slope * x)
        dim = input.shape[1]
        Wh = input
        Wh1 = Wh @ a[:dim, :]
        Wh2 = Wh @ a[dim:, :]
        e = leaky_relu(Wh1 + Wh2.T)
        e = jnp.where(adj_matrix > 0, e, NEG_BIG)
        attention = jax.nn.softmax(e, axis=1)
        return attention @ Wh

    def _L1_gnn_ref(prop_state, A, in_W, in_b, out_W, out_b, r_W, r_b, z_W, z_b, h_W, h_b, o1_W, o1_b, o2_W, o2_b):
        import jax, jax.numpy as jnp
        import numpy as np
        N = 2048
        STATE_DIM = 256
        OUTPUT_DIM = 256
        N_STEPS = 5
        W_STD = 0.02

        def _lin_params(key, out_dim, in_dim):
            W = jax.random.normal(key, (out_dim, in_dim), dtype=jnp.float32) * W_STD
            b = jnp.zeros((out_dim,), dtype=jnp.float32)
            return (W, b)
        Af = A.astype(prop_state.dtype)
        AfT = Af.T
        state = prop_state
        for _ in range(N_STEPS):
            s_in = state @ in_W.T + in_b
            s_out = state @ out_W.T + out_b
            a_in = Af @ s_in
            a_out = AfT @ s_out
            a = jnp.concatenate([a_in, a_out, state], axis=-1)
            r = jax.nn.sigmoid(a @ r_W.T + r_b)
            z = jax.nn.sigmoid(a @ z_W.T + z_b)
            joined = jnp.concatenate([a_in, a_out, r * state], axis=-1)
            h_hat = jnp.tanh(joined @ h_W.T + h_b)
            state = (1.0 - z) * state + z * h_hat
        out = jnp.tanh(state @ o1_W.T + o1_b) @ o2_W.T + o2_b
        return out
    h = jnp.maximum(_layernorm(x, axis=-1), 0.0)
    x = x + _L0_gnn_ref(h, adj, L0_gnn_a)
    h = jnp.maximum(_layernorm(x, axis=-1), 0.0)
    x = x + _L1_gnn_ref(h, adj, L1_gnn_in_W, L1_gnn_in_b, L1_gnn_out_W, L1_gnn_out_b, L1_gnn_r_W, L1_gnn_r_b, L1_gnn_z_W, L1_gnn_z_b, L1_gnn_h_W, L1_gnn_h_b, L1_gnn_o1_W, L1_gnn_o1_b, L1_gnn_o2_W, L1_gnn_o2_b)
    return x

_drawn_inputs = setup_inputs


def setup_inputs(seed=0):
    import zlib

    import numpy as np

    out = dict(_drawn_inputs(seed))
    spreads = {'L1_gnn_in_b': (0.0, 0.1),
     'L1_gnn_out_b': (0.0, 0.1),
     'L1_gnn_r_b': (0.0, 2.0),
     'L1_gnn_z_b': (0.0, 2.0),
     'L1_gnn_h_b': (0.0, 0.8),
     'L1_gnn_o1_b': (0.0, 0.1),
     'L1_gnn_o2_b': (0.0, 0.1)}
    factors = {'L1_gnn_r_W': 64.0}
    for name, (base, spread) in spreads.items():
        noise = np.random.default_rng([zlib.crc32(name.encode()), seed]).standard_normal(out[name].shape)
        drawn = base * np.exp(spread * noise) if base else spread * noise
        out[name] = jnp.asarray(drawn.astype(out[name].dtype))
    for name, factor in factors.items():
        out[name] = (out[name] * factor).astype(out[name].dtype)
    return out
```

```python
from contextlib import ExitStack

import concourse.bass as bass
from concourse import mybir

ALU = mybir.AluOpType
ACT = mybir.ActivationFunctionType
F32 = mybir.dt.float32
F32R = mybir.dt.float32r
I32 = mybir.dt.int32

P = 128
BANK = 512
STEPS = 5
EPS = 1e-5
NEG_BIG = 9000000000000000.0
SLOTS = 11264

Z, R, H = 0, 1, 2


def gat_ggnn_kernel(nc, x, adj, a, in_W, in_b, out_W, out_b, r_W, r_b, z_W, z_b, h_W, h_b,
                    o1_W, o1_b, o2_W, o2_b, out):
    N, DIM = x.shape
    assert DIM == 2 * P and N % 2 == 0
    NT = -(-N // P)
    LAST = N - (NT - 1) * P
    rows = [P] * (NT - 1) + [LAST]
    FT = NT - 1
    G3 = 3 * DIM
    TPC = BANK // P
    starts = list(range(0, N, BANK))
    chunks = [(c0, min(BANK, N - c0)) for c0 in starts]
    NC = len(chunks)
    LC = NC - 1
    assert NC == 3
    chunk_tiles = [[t for t in range(NT) if t * P // BANK == c] for c in range(NC)]
    early_tiles = [t for t in range(NT) if t * P // BANK < LC]
    late_tiles = chunk_tiles[LC]

    x1_dram = nc.dram_tensor("x1_scratch", (N, DIM), F32).ap()
    degree_in_dram = nc.dram_tensor("degree_in_scratch", (2, NT * P), F32).ap()
    degree_out_dram = nc.dram_tensor("degree_out_scratch", (2, N), F32).ap()
    bias_dram = nc.dram_tensor("bias_scratch", (6, G3), F32).ap()

    ctx = ExitStack()
    with ctx:
        base = -(-nc.sbuf_base // 32) * 32

        def place(name, shape, dtype, offset):
            words = 1
            for n in shape[1:]:
                words *= n
            offset += offset % 8
            assert base + offset + 4 * words <= nc.sbuf_usable_end, (name, offset)
            return nc.alloc_sbuf_tensor_at(name, shape, dtype, offset=base + offset, align_bytes=8), \
                offset + 4 * words

        A_rows, at = place("A_rows", [P, NT, N], F32R, 0)
        cols_at = at
        A_cols, at = place("A_cols", [P, NT, N], F32R, at)
        DEG, at = place("DEG", [P, N], F32R, at)
        BW, at = place("BW", [P, G3], F32R, at)
        ident, at = place("ident", [P, P], F32, at)
        arena = at
        W_hi, at = place("W_hi", [P, 6, G3], F32R, arena)
        W_lo, at = place("W_lo", [P, 6, G3], F32R, at)
        nodes_at = at
        S_hi, lo_at = place("S_hi", [P, NT, DIM], F32R, nodes_at)
        S_lo, at = place("S_lo", [P, NT, DIM], F32R, lo_at)
        ST, at = place("ST", [P, 2, N], F32, at)
        uv_at = at
        UV_hi, at = place("UV_hi", [P, 4, BANK], F32R, at)
        UV_lo, at = place("UV_lo", [P, 4, BANK], F32R, at)
        SC_hi, at = place("SC_hi", [P, 2, BANK], F32R, at)
        SC_lo, at = place("SC_lo", [P, 2, BANK], F32R, at)
        tmp, at = place("tmp", [P, 2, BANK], F32, at)
        A_int, at = place("A_int", [P, 2, N], I32, arena)
        scores, at = place("scores", [P, 2, N], F32, at)
        leaky, at = place("leaky", [P, 1, N], F32, at)
        b_row, at = place("b_row", [P, N], F32, at)
        A_sum, at = place("A_sum", [P, N], F32, nodes_at + 2 * NT * DIM * 4)
        degree_row, _ = place("degree_row", [1, 2, N], F32R, uv_at)
        PT, at = place("PT", [P, 2, NT, P], F32, nodes_at)
        h, at = place("h", [P, NT, DIM], F32, lo_at)
        W_f32, at = place("W_f32", [P, 6, G3], F32, uv_at)
        X, at = place("X", [P, NT, DIM], F32, at)
        degree_T, at = place("degree_T", [2 * NT, P], F32R, at)
        at = nodes_at + 2 * NT * DIM * 4 + 4 * N
        stats, at = place("stats", [P, 2, 6], F32, at)
        mean_var, at = place("mean_var", [P, NT, 2], F32, at)
        std, at = place("std", [P, NT], F32, at)
        rstd, at = place("rstd", [P, NT], F32, at)
        newton, at = place("newton", [P, NT], F32, at)
        a_col, at = place("a_col", [P, NT], F32, at)
        b_col, at = place("b_col", [P, NT], F32, at)
        row_max, at = place("row_max", [P, NT], F32, at)
        neg_max, at = place("neg_max", [P, NT], F32, at)
        row_sum, at = place("row_sum", [P, NT], F32, at)
        inv_sum, at = place("inv_sum", [P, NT], F32, at)
        degree_in, at = place("degree_in", [P, NT], F32, at)
        degree_pair, at = place("degree_pair", [P, 2, NT], F32R, at)
        ones, at = place("ones", [P, 2], F32, at)
        product, at = place("product", [P, DIM], F32, at)
        assert at <= uv_at
        gate_nat, at = place("gate_nat", [P, 3, 2, G3], F32, cols_at)
        gate_T, at = place("gate_T", [P, 4, G3], F32, at)
        msg_nat, at = place("msg_nat", [P, 2, 2, DIM], F32, at)
        bias_rows, at = place("bias_rows", [1, 6, G3], F32R, at)
        gate_bias, at = place("gate_bias", [1, G3], F32, at)
        msg_bias, at = place("msg_bias", [P, 2, 2], F32, at)
        a_bc, at = place("a_bc", [P, 2, DIM], F32, at)
        assert at <= 2 * cols_at
        o_nat, at = place("o_nat", [P, 2, 2, DIM], F32, 0)
        o_T, at = place("o_T", [P, 2, 2, DIM], F32, at)
        o1_bias, at = place("o1_bias", [P, 2], F32, at)
        o2_bias, at = place("o2_bias", [P, DIM], F32, at)
        x1_back, at = place("x1_back", [P, NT, DIM], F32, at)
        result, at = place("result", [P, NT, DIM], F32, at)
        assert at <= cols_at
        YT, at = place("YT", [P, 2, N], F32, cols_at)

        def f32(ap):
            return ap.bitcast(F32)

        uvp = ctx.enter_context(nc.psum_tensor("uvp", [P, 4, BANK], F32))
        gp = ctx.enter_context(nc.psum_tensor("gp", [P, 4, BANK], F32))

        def sem(name):
            return ctx.enter_context(nc.semaphore(name))

        x_in, a_in, gates_in, msg_in, bias_in = (sem(n) for n in
                                                 ("x_in", "a_in", "gates_in", "msg_in", "bias_in"))
        adj_in = [sem("adj_in_even"), sem("adj_in_odd")]
        x1_out, deg_out, bias_out = sem("x1_out"), sem("deg_out"), sem("bias_out")
        deg_in_sem, bw_in, o_in, x1_in, result_out = (sem(n) for n in
                                                      ("deg_in", "bw_in", "o_in", "x1_in", "result_out"))
        ident_ready, fill_ready = sem("ident_ready"), sem("fill_ready")
        var_ready, std_ready = sem("var_ready"), sem("std_ready")
        b_ready, b_full, b_copied, a_ready = sem("b_ready"), sem("b_full"), sem("b_copied"), sem("a_ready")
        wt_full, wt_copied = sem("wt_full"), sem("wt_copied")
        fused_full, fused_copied = sem("fused_full"), sem("fused_copied")
        bias_full, bias_hi, bias_split = sem("bias_full"), sem("bias_hi"), sem("bias_split")
        converted, summed = sem("converted"), sem("summed")
        at_full, at_copied = sem("at_full"), sem("at_copied")
        leaky_ready, score_ready, prob_ready = sem("leaky_ready"), sem("score_ready"), sem("prob_ready")
        pt_full, pt_copied = sem("pt_full"), sem("pt_copied")
        att_full, x1_ready = sem("att_full"), sem("x1_ready")
        w_hi_ready, w_ready = sem("w_hi_ready"), sem("w_ready")
        ln2_ready, ln2_T_full, st_ready = (sem(n) for n in
                                                        ("ln2_ready", "ln2_T_full", "st_ready"))
        degpair_ready, degT_full, degT_copied = sem("degpair_ready"), sem("degT_full"), sem("degT_copied")
        degrow_full, degrow_hi, degrow_ready = sem("degrow_full"), sem("degrow_hi"), sem("degrow_ready")
        uv_full, uv_hi, uv_ready = sem("uv_full"), sem("uv_hi"), sem("uv_ready")
        sc_ready = sem("sc_ready")
        r_full, r_act, r_used, rs_ready = sem("r_full"), sem("r_act"), sem("r_used"), sem("rs_ready")
        z_full, z_act, h_full, h_act = sem("z_full"), sem("z_act"), sem("h_full"), sem("h_act")
        updated = sem("updated")
        t_full, t_hi, t_ready = sem("t_full"), sem("t_hi"), sem("t_ready")
        oT_full, oT_copied, y_full, y_ready = sem("oT_full"), sem("oT_copied"), sem("y_full"), sem("y_ready")
        r_out_full, x1b_ready, result_ready = sem("r_out_full"), sem("x1b_ready"), sem("result_ready")
        dve_done, loop_done = sem("dve_done"), sem("loop_done")
        pool_done = sem("pool_done")

        ln2_banks = [uvp[:, 0, :], uvp[:, 1, :], uvp[:, 2, :], uvp[:, 3, :], gp[:, 3, :], uvp[:, 0, :]]
        fills = [list(range(q, min(q + TPC, NT))) for q in range(0, NT, TPC)]
        NF = len(fills)

        block = ctx.enter_context(nc.Block())

        @block.sync
        def _(sp):
            sp.dma_start(X[:, 0:FT, :], x[0:FT * P, :].rearrange("(t p) d -> p t d", p=P)).then_inc(x_in, 16)
            sp.dma_start(X[0:LAST, FT, :], x[FT * P:N, :]).then_inc(x_in, 16)
            sp.dma_start(a_bc[:, :, :].rearrange("p k d -> p (k d)"),
                         a.rearrange("k o -> o k").to_broadcast([P, 2 * DIM])).then_inc(a_in, 16)
            for g, w in ((Z, z_W), (R, r_W), (H, h_W)):
                sp.dma_start(gate_nat[:, g, :, :], w.rearrange("(c p) k -> p c k", p=P)).then_inc(gates_in, 16)
            for k, w in enumerate((in_W, out_W)):
                sp.dma_start(msg_nat[:, k, :, :], w.rearrange("(c p) k -> p c k", p=P)).then_inc(msg_in, 16)
            for g, b in ((Z, z_b), (R, r_b), (H, h_b)):
                sp.dma_start(gate_bias[0:1, g * DIM:(g + 1) * DIM],
                             b.rearrange("(o m) -> o m", o=1)).then_inc(bias_in, 16)
            with nc.allow_non_contiguous_dma(reason="256 biases, one to a partition"):
                for k, b in enumerate((in_b, out_b)):
                    sp.dma_start(msg_bias[:, k, :], b.rearrange("(c p) -> p c", p=P)).then_inc(bias_in, 16)
            for t in range(NT):
                if t >= 2:
                    sp.wait_ge(converted, t - 1)
                sp.dma_start(A_int[0:rows[t], t % 2, :],
                             adj[t * P:t * P + rows[t], :]).then_inc(adj_in[t % 2], 16)
                if t == 2:
                    sp.wait_ge(bias_split, 3)
                    sp.dma_start(bias_dram.rearrange("(o k) m -> o k m", o=1),
                                 f32(bias_rows[:, :, :])).then_inc(bias_out, 16)
                    sp.wait_ge(bias_out, 16)
                    sp.wait_ge(fill_ready, 2)
                    for k in range(2):
                        for twice in range(2):
                            sp.dma_start(f32(BW[4 * k + 2 * twice:4 * k + 2 * twice + 2, :]),
                                         bias_dram[2 * k:2 * k + 2, :]).then_inc(bw_in, 16)
                    sp.dma_start(f32(BW[8:10, :]), bias_dram[4:6, :]).then_inc(bw_in, 16)
            for t in range(NT):
                sp.wait_ge(x1_ready, t + 1)
                sp.dma_start(x1_dram[t * P:t * P + rows[t], :], X[0:rows[t], t, :]).then_inc(x1_out, 16)
            sp.wait_ge(degT_copied, 1)
            sp.dma_start(degree_in_dram.rearrange("k (t c) -> (k t) c", c=P), f32(degree_T[:, :])).then_inc(deg_out, 16)
            sp.wait_ge(degrow_ready, NF)
            sp.dma_start(degree_out_dram.rearrange("(o k) n -> o k n", o=1), f32(degree_row[:, :, :])).then_inc(deg_out, 16)
            sp.wait_ge(deg_out, 32)
            for k, src in enumerate((degree_in_dram, degree_out_dram)):
                for half in range(2):
                    r0 = 4 * k + 2 * half
                    sp.dma_start(f32(DEG[r0:r0 + 2, :]),
                                 src[half:half + 1, 0:N].to_broadcast([2, N])).then_inc(deg_in_sem, 16)
            sp.wait_ge(uv_full, 4 * NC * STEPS)
            for k, w in enumerate((o1_W, o2_W)):
                sp.dma_start(o_nat[:, k, :, :], w.rearrange("(c p) k -> p c k", p=P)).then_inc(o_in, 16)
            with nc.allow_non_contiguous_dma(reason="256 biases, one to a partition"):
                sp.dma_start(o1_bias[:, :], o1_b.rearrange("(c p) -> p c", p=P)).then_inc(o_in, 16)
            sp.dma_start(o2_bias[:, :], o2_b.rearrange("(o m) -> o m", o=1).to_broadcast([P, DIM])).then_inc(x1_in, 16)
            sp.dma_start(x1_back[:, 0:FT, :], x1_dram[0:FT * P, :].rearrange("(t p) d -> p t d", p=P)).then_inc(x1_in, 16)
            sp.dma_start(x1_back[0:LAST, FT, :], x1_dram[FT * P:N, :]).then_inc(x1_in, 16)
            n = 0
            for t in range(0, NT, 2):
                n += 1
                sp.wait_ge(result_ready, min(t + 2, NT))
                if t + 1 < FT:
                    sp.dma_start(out[t * P:(t + 2) * P, :].rearrange("(t p) d -> p t d", p=P),
                                 result[:, t:t + 2, :]).then_inc(result_out, 16)
                else:
                    sp.dma_start(out[t * P:t * P + rows[t], :], result[0:rows[t], t, :]).then_inc(result_out, 16)
                    if t + 1 < NT:
                        n += 1
                        sp.dma_start(out[FT * P:N, :], result[0:LAST, FT, :]).then_inc(result_out, 16)
            sp.wait_ge(result_out, 16 * n)
            sp.wait_ge(x1_out, 16 * NT)

        @block.gpsimd
        def _(pool):
            pool.memset(ident[:, :], 0.0).then_inc(pool_done, 1)
            pool.wait_ge(pool_done, 1)
            pool.affine_select(out=ident[:, :], in_=ident[:, :], compare_op=ALU.not_equal, fill=1.0,
                               base=0, pattern=[[-1, P]], channel_multiplier=1).then_inc(ident_ready, 1)
            pool.memset(ones[:, :], 1.0).then_inc(ident_ready, 1)
            pool.memset(f32(BW[:, :]), 0.0).then_inc(fill_ready, 1)
            pool.memset(f32(DEG[:, :]), 1.0).then_inc(fill_ready, 1)
            for t in range(NT):
                p = rows[t]
                pool.wait_ge(converted, t + 1)
                src = f32(A_rows[0:p, t, :])
                if t == 0:
                    pool.tensor_copy(A_sum[0:p, :], src).then_inc(summed, 1)
                else:
                    pool.wait_ge(summed, t)
                    pool.tensor_tensor(A_sum[0:p, :], A_sum[0:p, :], src, ALU.add).then_inc(summed, 1)

        @block.scalar
        def _(act):
            for f in range(9):
                g, pair = divmod(f, 3)
                act.wait_ge(wt_full, f + 1)
                dst = gate_T if pair < 2 else W_f32
                kk = 2 * pair if pair < 2 else 4
                act.activation(dst[:, kk:kk + 2, g * DIM:(g + 1) * DIM],
                               gp[:, f % 4, :].rearrange("p (k m) -> p k m", k=2), ACT.Copy).then_inc(wt_copied, 1)
            for kt in range(4):
                act.wait_ge(fused_full, 2 * kt + 1)
                act.activation(W_f32[:, kt, 0:BANK], uvp[:, kt, :], ACT.Copy).then_inc(fused_copied, 1)
                act.wait_ge(fused_full, 2 * kt + 2)
                act.activation(W_f32[:, kt, BANK:G3], gp[:, kt, 0:G3 - BANK], ACT.Copy).then_inc(fused_copied, 1)
            for k in range(3):
                if k < 2:
                    act.wait_ge(bias_full, 2 * k + 2)
                    act.activation(bias_rows[0:1, 2 * k, 0:BANK], uvp[0:1, 2 * k, :], ACT.Copy)
                    act.activation(bias_rows[0:1, 2 * k, BANK:G3], uvp[0:1, 2 * k + 1, 0:G3 - BANK],
                                   ACT.Copy).then_inc(bias_hi, 1)
                else:
                    act.wait_ge(bias_in, 16 * 5)
                    act.activation(bias_rows[0:1, 4, :], gate_bias[0:1, :], ACT.Copy).then_inc(bias_hi, 1)

            def convert(t):
                p = rows[t]
                act.wait_ge(adj_in[t % 2], 16 * (t // 2 + 1))
                act.activation(A_rows[0:p, t, :], A_int[0:p, t % 2, :], ACT.Copy,
                               accum_out=degree_in[0:p, t:t + 1]).then_inc(converted, 1)

            act.wait_ge(var_ready, 1)
            act.activation(std[:, :], mean_var[:, :, 1], ACT.Sqrt).then_inc(std_ready, 1)
            convert(0)
            convert(1)
            for q, tiles in enumerate(fills):
                n = min(N, (tiles[-1] + 1) * P) - tiles[0] * P
                act.wait_ge(b_full, q + 1)
                act.activation(b_row[:, tiles[0] * P:tiles[0] * P + n], uvp[:, q, 0:n], ACT.Copy).then_inc(b_copied, 1)

            def leaky_scores(t):
                if t >= 1:
                    act.wait_ge(score_ready, t)
                act.activation(leaky[0:rows[t], 0, :], b_row[0:rows[t], :], ACT.Identity,
                               bias=a_col[0:rows[t], t:t + 1]).then_inc(leaky_ready, 1)

            act.wait_ge(b_copied, NF)
            act.wait_ge(a_ready, 1)
            leaky_scores(0)
            for t in range(NT):
                p = rows[t]
                if t + 1 < NT:
                    leaky_scores(t + 1)
                act.wait_ge(score_ready, t + 1)
                act.activation(scores[0:p, t % 2, :], scores[0:p, t % 2, :], ACT.Exp,
                               bias=neg_max[0:p, t:t + 1],
                               accum_out=row_sum[0:p, t:t + 1]).then_inc(prob_ready, 1)
                if t + 2 < NT:
                    convert(t + 2)
                if t >= 2:
                    act.wait_ge(att_full, t - 1)
                for q, tiles in enumerate(fills):
                    act.wait_ge(pt_full, NF * t + q + 1)
                    full = [k for k in tiles if k < FT]
                    last = act.activation(PT[:, t % 2, full[0]:full[-1] + 1, 0:p],
                                          uvp[:, q, 0:len(full) * P].rearrange("p (k i) -> p k i", i=P)[:, :, 0:p],
                                          ACT.Copy)
                    if FT in tiles:
                        last = act.activation(PT[0:LAST, t % 2, FT, 0:p],
                                              uvp[0:LAST, q, (FT - tiles[0]) * P:(FT - tiles[0]) * P + p],
                                              ACT.Copy)
                    last.then_inc(pt_copied, 1)
            act.wait_ge(pt_full, NF * NT)
            act.wait_ge(score_ready, NT)
            act.wait_ge(at_copied, NF * NT)
            for g in range(3):
                act.activation(W_hi[:, :, g * DIM:(g + 1) * DIM], W_f32[:, :, g * DIM:(g + 1) * DIM],
                               ACT.Copy).then_inc(w_hi_ready, 1)
            act.wait_ge(var_ready, 2)
            act.activation(std[:, :], mean_var[:, :, 1], ACT.Sqrt).then_inc(std_ready, 1)
            act.wait_ge(degT_full, 1)
            act.activation(degree_T[:, :], gp[0:2 * NT, 3, 0:P], ACT.Copy).then_inc(degT_copied, 1)
            act.wait_ge(degrow_full, NC)
            for f in range(2 * NC):
                c, m = divmod(f, 2)
                c0, n = chunks[c]
                bank = ln2_banks[f][:, 0:n]
                act.wait_ge(ln2_T_full, f + 1)
                act.activation(ST[:, m, c0:c0 + n], bank, ACT.Relu).then_inc(st_ready, 1)
            act.wait_ge(w_ready, 3)
            for c, (c0, n) in enumerate(chunks):
                act.wait_ge(degrow_full, c + 1)
                act.activation(degree_row[0:1, 0, c0:c0 + n], gp[0:1, c, 0:n], ACT.Copy).then_inc(degrow_hi, 1)
            act.wait_ge(deg_out, 32)

            with act.Fori(0, STEPS) as step:
                def state_hi(k, bank, t0, count, p):
                    act.wait_ge(t_full, step * 6 + k + 1)
                    act.activation(S_hi[0:p, t0:t0 + count, :],
                                   bank[0:p, 0:count * DIM].rearrange("p (t d) -> p t d", d=DIM),
                                   ACT.Copy).then_inc(t_hi, 1)

                state_hi(0, gp[:, 2, :], late_tiles[0], len(late_tiles) - 1, P)
                state_hi(1, gp[:, 3, :], FT, 1, LAST)
                for c, (c0, n) in enumerate(chunks):
                    for b in range(4):
                        act.wait_ge(uv_full, step * 12 + 4 * c + b + 1)
                        act.activation(UV_hi[:, b, 0:n], uvp[:, b, 0:n], ACT.Copy).then_inc(uv_hi, 1)
                    for m in range(2):
                        act.wait_ge(r_full, step * 6 + 2 * c + m + 1)
                        act.activation(gp[:, m, 0:n], gp[:, m, 0:n], ACT.Sigmoid).then_inc(r_act, 1)
                    if c == LC:
                        for k in range(4):
                            state_hi(2 + k, uvp[:, k, :], 2 * k, 2, P)
                    for m in range(2):
                        act.wait_ge(z_full, step * 6 + 2 * c + m + 1)
                        act.activation(gp[:, 2 + m, 0:n], gp[:, 2 + m, 0:n], ACT.Sigmoid).then_inc(z_act, 1)
                    for m in range(2):
                        act.wait_ge(h_full, step * 6 + 2 * c + m + 1)
                        act.activation(gp[:, m, 0:n], gp[:, m, 0:n], ACT.Tanh).then_inc(h_act, 1)

            for k in range(2):
                act.wait_ge(oT_full, k + 1)
                act.activation(o_T[:, k, :, :], uvp[:, k, :].rearrange("p (c m) -> p c m", c=2),
                               ACT.Copy).then_inc(oT_copied, 1)
            for f in range(2 * NC):
                c, m = divmod(f, 2)
                c0, n = chunks[c]
                act.wait_ge(y_full, f + 1)
                act.activation(YT[:, m, c0:c0 + n], gp[:, f % 4, 0:n], ACT.Tanh,
                               bias=o1_bias[:, m:m + 1]).then_inc(y_ready, 1)

        @block.vector
        def _(dve):
            chain = [0]

            def then(instruction):
                chain[0] += 1
                instruction.then_inc(dve_done, 1)
                dve.wait_ge(dve_done, chain[0])

            def statistics(t):
                p = rows[t]
                then(dve.bn_stats(stats[0:p, t % 2, :], X[0:p, t, :]))
                then(dve.bn_aggr(mean_var[0:p, t, :], stats[0:p, t % 2, :]))

            def reciprocal_deviation(turn):
                dve.tensor_scalar(mean_var[:, :, 1], mean_var[:, :, 1], EPS, None, ALU.add).then_inc(var_ready, 1)
                dve.wait_ge(std_ready, turn)
                then(dve.reciprocal(rstd[:, :], std[:, :]))
                then(dve.tensor_tensor(newton[:, :], rstd[:, :], rstd[:, :], ALU.mult))
                then(dve.tensor_tensor(newton[:, :], newton[:, :], mean_var[:, :, 1], ALU.mult))
                then(dve.tensor_scalar(newton[:, :], newton[:, :], -0.5, 1.5, ALU.mult, ALU.add))
                then(dve.tensor_tensor(rstd[:, :], rstd[:, :], newton[:, :], ALU.mult))

            def normalise(t):
                p = rows[t]
                return dve.tensor_scalar(h[0:p, t, :], X[0:p, t, :], mean_var[0:p, t, 0:1], rstd[0:p, t:t + 1],
                                         ALU.subtract, ALU.mult)

            then(dve.memset(mean_var[:, :, :], 1.0))
            then(dve.memset(degree_in[:, :], 0.0))
            dve.wait_ge(x_in, 32)
            for t in range(NT):
                statistics(t)
            reciprocal_deviation(1)
            for t in range(NT):
                last = normalise(t)
            then(last)
            dve.tensor_scalar(h[:, 0:FT, :], h[:, 0:FT, :], 0.0, None, ALU.max)
            then(dve.tensor_scalar(h[0:LAST, FT, :], h[0:LAST, FT, :], 0.0, None, ALU.max))
            dve.wait_ge(a_in, 16)
            for half, col, ready in ((1, b_col, b_ready), (0, a_col, a_ready)):
                for t in range(NT):
                    p = rows[t]
                    last = dve.tensor_tensor_reduce(product[0:p, :], h[0:p, t, :], a_bc[0:p, half, :], 1.0, 0.0,
                                                    ALU.mult, ALU.add, col[0:p, t:t + 1])
                    if t < NT - 1:
                        then(last)
                last.then_inc(ready, 1)
                dve.wait_ge(ready, 1)
            dve.wait_ge(bias_full, 4)
            for k in range(3):
                dve.wait_ge(bias_hi, k + 1)
                if k < 2:
                    dve.tensor_tensor(bias_rows[0:1, 2 * k + 1, 0:BANK], uvp[0:1, 2 * k, :],
                                      f32(bias_rows[0:1, 2 * k, 0:BANK]), ALU.subtract)
                    last = dve.tensor_tensor(bias_rows[0:1, 2 * k + 1, BANK:G3], uvp[0:1, 2 * k + 1, 0:G3 - BANK],
                                             f32(bias_rows[0:1, 2 * k, BANK:G3]), ALU.subtract)
                else:
                    last = dve.tensor_tensor(bias_rows[0:1, 5, :], gate_bias[0:1, :],
                                             f32(bias_rows[0:1, 4, :]), ALU.subtract)
                last.then_inc(bias_split, 1)

            def columns(t):
                p = rows[t]
                if t == 0:
                    dve.wait_ge(fused_copied, 8)
                    dve.wait_ge(bias_out, 16)
                for q, tiles in enumerate(fills):
                    dve.wait_ge(at_full, NF * t + q + 1)
                    full = [k for k in tiles if k < FT]
                    last = dve.tensor_copy(A_cols[:, full[0]:full[-1] + 1, t * P:t * P + p],
                                           gp[:, q, 0:len(full) * P].rearrange("p (k i) -> p k i", i=P)[:, :, 0:p])
                    if FT in tiles:
                        last = dve.tensor_copy(A_cols[0:LAST, FT, t * P:t * P + p],
                                               gp[0:LAST, q, (FT - tiles[0]) * P:(FT - tiles[0]) * P + p])
                    last.then_inc(at_copied, 1)

            def score(t):
                p = rows[t]
                s = scores[0:p, t % 2, :]
                if t == 0:
                    dve.wait_ge(converted, 1)
                if t >= 2:
                    dve.wait_ge(pt_full, NF * (t - 1))
                then(dve.tensor_scalar(s, f32(A_rows[0:p, t, :]), 0.0, NEG_BIG, ALU.is_le, ALU.mult))
                dve.wait_ge(leaky_ready, t + 1)
                then(dve.scalar_tensor_tensor(leaky[0:p, 0, :], leaky[0:p, 0, :], 0.01, leaky[0:p, 0, :],
                                              ALU.mult, ALU.max))
                then(dve.tensor_tensor_reduce(s, leaky[0:p, 0, :], s, 1.0, -3.0e38,
                                              ALU.subtract, ALU.max, row_max[0:p, t:t + 1]))
                dve.tensor_scalar(neg_max[0:p, t:t + 1], row_max[0:p, t:t + 1], -1.0, None,
                                  ALU.mult).then_inc(score_ready, 1)

            def residual(t):
                p = rows[t]
                bank = uvp[0:p, 3, 0:DIM] if t % 2 == 0 else gp[0:p, 3, 0:DIM]
                dve.wait_ge(prob_ready, t + 1)
                then(dve.reciprocal(inv_sum[0:p, t:t + 1], row_sum[0:p, t:t + 1]))
                dve.wait_ge(att_full, t + 1)
                last = dve.scalar_tensor_tensor(X[0:p, t, :], bank, inv_sum[0:p, t:t + 1], X[0:p, t, :],
                                                ALU.mult, ALU.add)
                last.then_inc(x1_ready, 1)
                dve.wait_ge(x1_ready, t + 1)
                statistics(t)

            columns(0)
            columns(1)
            score(0)
            for t in range(NT):
                if t + 1 < NT:
                    if t + 1 >= 1:
                        dve.wait_ge(converted, t + 2)
                    score(t + 1)
                if t + 2 < NT:
                    columns(t + 2)
                if t >= 1:
                    residual(t - 1)
            dve.wait_ge(converted, NT)
            then(dve.tensor_copy(degree_pair[:, 0, :], degree_in[:, :]))
            dve.tensor_tensor(degree_pair[:, 1, :], degree_in[:, :], f32(degree_pair[:, 0, :]),
                              ALU.subtract).then_inc(degpair_ready, 1)
            residual(NT - 1)
            reciprocal_deviation(2)
            dve.wait_ge(att_full, NT)
            for t in range(NT):
                last = normalise(t)
            then(last)
            early = len(early_tiles)
            dve.tensor_scalar(S_hi[:, 0:early, :], h[:, 0:early, :], 0.0, None, ALU.max).then_inc(ln2_ready, 1)
            for g in range(3):
                cols = slice(g * DIM, (g + 1) * DIM)
                dve.wait_ge(w_hi_ready, g + 1)
                dve.tensor_tensor(W_lo[:, :, cols], W_f32[:, :, cols], f32(W_hi[:, :, cols]),
                                  ALU.subtract).then_inc(w_ready, 1)
            dve.wait_ge(ln2_T_full, 2 * NC)
            dve.wait_ge(ln2_ready, 1)
            dve.scalar_tensor_tensor(S_lo[:, 0:early, :], h[:, 0:early, :], 0.0, f32(S_hi[:, 0:early, :]),
                                     ALU.max, ALU.subtract).then_inc(t_ready, 1)
            for c, (c0, n) in enumerate(chunks):
                dve.wait_ge(degrow_hi, c + 1)
                dve.tensor_tensor(degree_row[0:1, 1, c0:c0 + n], gp[0:1, c, 0:n],
                                  f32(degree_row[0:1, 0, c0:c0 + n]), ALU.subtract).then_inc(degrow_ready, 1)
            dve.wait_ge(x1_out, 16 * NT)
            dve.wait_ge(st_ready, 2 * NC)
            dve.memset(tmp[0:1, 0, 0:2], 0.0).then_inc(updated, 1)
            dve.wait_ge(deg_out, 32)

            with dve.Fori(0, STEPS) as step:
                links = [0]
                per_step = 7 * NC

                def link(instruction):
                    links[0] += 1
                    instruction.then_inc(loop_done, 1)
                    dve.wait_ge(loop_done, step * per_step + links[0])

                def split_chunk(c):
                    c0, n = chunks[c]
                    link(dve.tensor_copy(SC_hi[:, :, 0:n], ST[:, :, c0:c0 + n]))
                    dve.tensor_tensor(SC_lo[:, :, 0:n], ST[:, :, c0:c0 + n], f32(SC_hi[:, :, 0:n]),
                                      ALU.subtract).then_inc(sc_ready, 1)

                def state_lo(k, bank, t0, count, p):
                    dve.wait_ge(t_hi, step * 6 + k + 1)
                    dve.tensor_tensor(S_lo[0:p, t0:t0 + count, :],
                                      bank[0:p, 0:count * DIM].rearrange("p (t d) -> p t d", d=DIM),
                                      f32(S_hi[0:p, t0:t0 + count, :]), ALU.subtract).then_inc(t_ready, 1)

                split_chunk(0)
                state_lo(0, gp[:, 2, :], late_tiles[0], len(late_tiles) - 1, P)
                state_lo(1, gp[:, 3, :], FT, 1, LAST)
                for c, (c0, n) in enumerate(chunks):
                    for b in range(4):
                        dve.wait_ge(uv_hi, step * 12 + 4 * c + b + 1)
                        dve.tensor_tensor(UV_lo[:, b, 0:n], uvp[:, b, 0:n], f32(UV_hi[:, b, 0:n]),
                                          ALU.subtract).then_inc(uv_ready, 1)
                    for m in range(2):
                        dve.wait_ge(r_act, step * 6 + 2 * c + m + 1)
                        ins = dve.tensor_tensor(tmp[:, m, 0:n], gp[:, m, 0:n], ST[:, m, c0:c0 + n], ALU.mult)
                        ins.then_inc(r_used, 1)
                        dve.wait_ge(r_used, step * 6 + 2 * c + m + 1)
                        link(dve.tensor_copy(SC_hi[:, m, 0:n], tmp[:, m, 0:n]))
                        dve.tensor_tensor(SC_lo[:, m, 0:n], tmp[:, m, 0:n], f32(SC_hi[:, m, 0:n]),
                                          ALU.subtract).then_inc(rs_ready, 1)
                    if c == LC:
                        for k in range(4):
                            state_lo(2 + k, uvp[:, k, :], 2 * k, 2, P)
                    for m in range(2):
                        dve.wait_ge(h_act, step * 6 + 2 * c + m + 1)
                        if m == 0:
                            dve.wait_ge(rs_ready, step * 6 + 2 * c + 2)
                        link(dve.tensor_tensor(tmp[:, m, 0:n], gp[:, m, 0:n], ST[:, m, c0:c0 + n], ALU.subtract))
                        dve.wait_ge(z_act, step * 6 + 2 * c + m + 1)
                        link(dve.tensor_tensor(tmp[:, m, 0:n], gp[:, 2 + m, 0:n], tmp[:, m, 0:n], ALU.mult))
                        dve.tensor_tensor(ST[:, m, c0:c0 + n], ST[:, m, c0:c0 + n], tmp[:, m, 0:n],
                                          ALU.add).then_inc(updated, 1)
                    dve.wait_ge(updated, step * 6 + 2 * c + 3)
                    if c < LC:
                        split_chunk(c + 1)
                assert links[0] == per_step

            dve.wait_ge(x1_in, 48)
            for t in range(NT):
                p = rows[t]
                last = dve.tensor_tensor(x1_back[0:p, t, :], x1_back[0:p, t, :], o2_bias[0:p, :], ALU.add)
            last.then_inc(x1b_ready, 1)
            dve.wait_ge(x1b_ready, 1)
            for t in range(NT):
                p = rows[t]
                dve.wait_ge(r_out_full, t + 1)
                dve.tensor_tensor(result[0:p, t, :], uvp[0:p, t % 4, 0:DIM], x1_back[0:p, t, :],
                                  ALU.add).then_inc(result_ready, 1)

        @block.tensor
        def _(pe):
            pe.wait_ge(ident_ready, 2)
            pe.wait_ge(gates_in, 48)
            for f in range(9):
                g, pair = divmod(f, 3)
                if f >= 4:
                    pe.wait_ge(wt_copied, f - 3)
                for kk in range(2):
                    for m in range(2):
                        k0 = (2 * pair + kk) * P
                        last = pe.transpose(gp[:, f % 4, kk * DIM + m * P:kk * DIM + (m + 1) * P],
                                            gate_nat[:, g, m, k0:k0 + P], ident[:, :])
                last.then_inc(wt_full, 1)
            pe.wait_ge(msg_in, 32)
            pe.wait_ge(wt_copied, 9)
            for kt in range(4):
                k, half = divmod(kt, 2)
                for bank, c0, n in ((uvp, 0, BANK), (gp, BANK, G3 - BANK)):
                    for tt in range(2):
                        last = pe.matmul(bank[:, kt, 0:n], msg_nat[:, k, tt, half * P:(half + 1) * P],
                                         gate_T[:, 2 * k + tt, c0:c0 + n], start=(tt == 0), stop=(tt == 1))
                    last.then_inc(fused_full, 1)
            pe.wait_ge(bias_in, 16 * 5)
            pe.wait_ge(fused_copied, 8)
            for k in range(2):
                for b, c0, n in ((2 * k, 0, BANK), (2 * k + 1, BANK, G3 - BANK)):
                    for tt in range(2):
                        last = pe.matmul(uvp[0:1, b, 0:n], msg_bias[:, k, tt:tt + 1],
                                         gate_T[:, 2 * k + tt, c0:c0 + n], start=(tt == 0), stop=(tt == 1))
                    last.then_inc(bias_full, 1)
            pe.wait_ge(b_ready, 1)
            pe.wait_ge(bias_split, 3)
            for q, tiles in enumerate(fills):
                for t in tiles:
                    p = rows[t]
                    last = pe.matmul(uvp[:, q, (t - tiles[0]) * P:(t - tiles[0]) * P + p],
                                     b_col[0:p, t:t + 1].to_broadcast([p, P]), ident[0:p, 0:p],
                                     start=True, stop=True)
                last.then_inc(b_full, 1)

            def transpose_adjacency(t):
                p = rows[t]
                pe.wait_ge(converted, t + 1)
                for q, tiles in enumerate(fills):
                    if t >= 1:
                        pe.wait_ge(at_copied, NF * (t - 1) + q + 1)
                    for k in tiles:
                        last = pe.transpose(gp[0:rows[k], q, (k - tiles[0]) * P:(k - tiles[0]) * P + p],
                                            f32(A_rows[0:p, t, k * P:k * P + rows[k]]), ident[0:p, 0:p])
                    last.then_inc(at_full, 1)

            transpose_adjacency(0)
            transpose_adjacency(1)
            for t in range(NT):
                p = rows[t]
                pe.wait_ge(prob_ready, t + 1)
                if t == 0:
                    pe.wait_ge(b_copied, NF)
                for q, tiles in enumerate(fills):
                    if t >= 1:
                        pe.wait_ge(pt_copied, NF * (t - 1) + q + 1)
                    for k in tiles:
                        last = pe.transpose(uvp[0:rows[k], q, (k - tiles[0]) * P:(k - tiles[0]) * P + p],
                                            scores[0:p, t % 2, k * P:k * P + rows[k]], ident[0:p, 0:p])
                    last.then_inc(pt_full, 1)
                if t + 2 < NT:
                    transpose_adjacency(t + 2)
                if t >= 2:
                    pe.wait_ge(x1_ready, t - 1)
                bank = uvp[0:p, 3, 0:DIM] if t % 2 == 0 else gp[0:p, 3, 0:DIM]
                for k in range(NT):
                    if k % TPC == 0:
                        pe.wait_ge(pt_copied, NF * t + k // TPC + 1)
                    last = pe.matmul(bank, PT[0:rows[k], t % 2, k, 0:p], h[0:rows[k], k, :],
                                     start=(k == 0), stop=(k == NT - 1))
                last.then_inc(att_full, 1)
            pe.wait_ge(summed, NT)
            pe.wait_ge(at_copied, NF * NT)
            for c, (c0, n) in enumerate(chunks):
                pe.matmul(gp[0:1, c, 0:n], ones[:, 0:1], A_sum[:, c0:c0 + n],
                          start=True, stop=True).then_inc(degrow_full, 1)
            pe.wait_ge(degpair_ready, 1)
            pe.wait_ge(x1_ready, NT)
            pe.transpose(gp[0:2 * NT, 3, 0:P], f32(degree_pair[:, :, :]).rearrange("p k t -> p (k t)"),
                         ident[:, :]).then_inc(degT_full, 1)
            pe.wait_ge(ln2_ready, 1)
            for f in range(2 * NC):
                c, m = divmod(f, 2)
                bank = ln2_banks[f]
                if f == 4:
                    pe.wait_ge(degT_copied, 1)
                if f == 5:
                    pe.wait_ge(st_ready, 1)
                for t in chunk_tiles[c]:
                    p = rows[t]
                    i0 = t * P - chunks[c][0]
                    last = pe.transpose(bank[:, i0:i0 + p], h[0:p, t, m * P:(m + 1) * P], ident[0:p, 0:p])
                last.then_inc(ln2_T_full, 1)
            pe.wait_ge(st_ready, 2 * NC)
            pe.wait_ge(bw_in, 16 * 5)

            with pe.Fori(0, STEPS) as step:
                def propagate(b, c, tiles, first, final):
                    c0, n = chunks[c]
                    m = b % 2
                    A = A_cols if b < 2 else A_rows
                    for t in tiles:
                        p = rows[t]
                        for part in (S_hi, S_lo):
                            ins = pe.matmul(uvp[:, b, 0:n], part[0:p, t, m * P:(m + 1) * P], A[0:p, t, c0:c0 + n],
                                            start=(first and t == tiles[0] and part is S_hi),
                                            stop=(final and t == tiles[-1] and part is S_lo))
                    if final:
                        ins.then_inc(uv_full, 1)

                def transpose_state(bank, tiles, column=0):
                    for i, t in enumerate(tiles):
                        p = rows[t]
                        for m in range(2):
                            ins = pe.transpose(bank[0:p, i * DIM + m * P:i * DIM + (m + 1) * P],
                                               ST[:, m, t * P:t * P + p], ident[:, :])
                    ins.then_inc(t_full, 1)

                def gate(bank, n, g, m, operands, first, final):
                    cols = slice(g * DIM + m * P, g * DIM + (m + 1) * P)
                    for i, (kt, hi, lo) in enumerate(operands):
                        for j, (w, v) in enumerate(((W_hi, hi), (W_hi, lo), (W_lo, hi))):
                            ins = pe.matmul(bank, w[:, kt, cols], v, start=(first and i == 0 and j == 0),
                                            stop=(final and i == len(operands) - 1 and j == 2))
                    return ins

                pe.wait_ge(t_ready, step * 6 + 1)
                for b in range(4):
                    propagate(b, 0, early_tiles, True, False)
                pe.wait_ge(updated, step * 6 + 1)
                pe.wait_ge(degrow_ready, NC)
                transpose_state(gp[:, 2, :], late_tiles[:-1])
                transpose_state(gp[:, 3, :], late_tiles[-1:])
                pe.wait_ge(t_ready, step * 6 + 3)
                for c, (c0, n) in enumerate(chunks):
                    for b in range(4):
                        if c == 0:
                            propagate(b, 0, late_tiles, False, True)
                        else:
                            pe.wait_ge(uv_ready, step * 12 + 4 * (c - 1) + b + 1)
                            propagate(b, c, list(range(NT)), True, True)
                    state = [(4 + k, SC_hi[:, k, 0:n], SC_lo[:, k, 0:n]) for k in range(2)]
                    message = [(k, UV_hi[:, k, 0:n], UV_lo[:, k, 0:n]) for k in range(4)]
                    pe.wait_ge(sc_ready, step * 3 + c + 1)
                    if c == 0:
                        pe.wait_ge(w_ready, 3)
                        pe.wait_ge(deg_in_sem, 16 * 4)
                    if c > 0:
                        pe.wait_ge(updated, step * 6 + 2 * c + 1)
                    for g, b0 in ((R, 0), (Z, 2)):
                        for m in range(2):
                            bank = gp[:, b0 + m, 0:n]
                            cols = slice(g * DIM + m * P, g * DIM + (m + 1) * P)
                            pe.matmul(bank, BW[:, cols], DEG[:, c0:c0 + n], start=True, stop=False)
                            gate(bank, n, g, m, state, False, False)
                    pe.wait_ge(uv_ready, step * 12 + 4 * (c + 1))
                    for m in range(2):
                        gate(gp[:, m, 0:n], n, R, m, message, False, True).then_inc(r_full, 1)
                    if c == LC:
                        for k in range(4):
                            transpose_state(uvp[:, k, :], [2 * k, 2 * k + 1])
                    for m in range(2):
                        gate(gp[:, 2 + m, 0:n], n, Z, m, message, False, True).then_inc(z_full, 1)
                    for m in range(2):
                        cols = slice(H * DIM + m * P, H * DIM + (m + 1) * P)
                        pe.wait_ge(r_used, step * 6 + 2 * c + m + 1)
                        pe.matmul(gp[:, m, 0:n], BW[:, cols], DEG[:, c0:c0 + n], start=True, stop=False)
                        gate(gp[:, m, 0:n], n, H, m, message, False, False)
                    pe.wait_ge(rs_ready, step * 6 + 2 * c + 2)
                    for m in range(2):
                        gate(gp[:, m, 0:n], n, H, m, state, False, True).then_inc(h_full, 1)

            pe.wait_ge(o_in, 48)
            pe.wait_ge(t_ready, 6 * STEPS + 1)
            for k in range(2):
                for c in range(2):
                    for m in range(2):
                        last = pe.transpose(uvp[:, k, c * DIM + m * P:c * DIM + (m + 1) * P],
                                            o_nat[:, k, m, c * P:(c + 1) * P], ident[:, :])
                last.then_inc(oT_full, 1)
            pe.wait_ge(oT_copied, 2)
            pe.wait_ge(updated, 6 * STEPS + 1)
            for f in range(2 * NC):
                c, m = divmod(f, 2)
                c0, n = chunks[c]
                if f >= 4:
                    pe.wait_ge(y_ready, f - 3)
                for k in range(2):
                    last = pe.matmul(gp[:, f % 4, 0:n], o_T[:, 0, k, m * P:(m + 1) * P], ST[:, k, c0:c0 + n],
                                     start=(k == 0), stop=(k == 1))
                last.then_inc(y_full, 1)
            for t in range(NT):
                p = rows[t]
                pe.wait_ge(y_ready, 2 * (t * P // BANK) + 2)
                if t >= 4:
                    pe.wait_ge(result_ready, t - 3)
                for k in range(2):
                    last = pe.matmul(uvp[0:p, t % 4, 0:DIM], YT[:, k, t * P:t * P + p], o_T[:, 1, k, :],
                                     start=(k == 0), stop=(k == 1))
                last.then_inc(r_out_full, 1)


_INS = ['x', 'adj', 'L0_gnn_a', 'L1_gnn_in_W', 'L1_gnn_in_b', 'L1_gnn_out_W', 'L1_gnn_out_b', 'L1_gnn_r_W',
        'L1_gnn_r_b', 'L1_gnn_z_W', 'L1_gnn_z_b', 'L1_gnn_h_W', 'L1_gnn_h_b', 'L1_gnn_o1_W', 'L1_gnn_o1_b',
        'L1_gnn_o2_W', 'L1_gnn_o2_b']


def kernel(**inputs):
    import numpy as _np
    import concourse.bacc as _bacc
    from concourse import mybir as _mybir
    from concourse.bass_utils import run_bass_kernel_spmd as _run

    nc = _bacc.Bacc("TRN2", target_bir_lowering=False, num_devices=1, dynamic_dma_scratch_size=256)
    arrays, args = {}, []
    for name in _INS:
        a = _np.ascontiguousarray(inputs[name])
        arrays[f"in_{name}_dram"] = a
        args.append(nc.dram_tensor(f"in_{name}_dram", a.shape, _mybir.dt.from_np(a.dtype), kind="ExternalInput").ap())
    args.append(nc.dram_tensor("out_0_dram", inputs['x'].shape, _mybir.dt.float32, kind="ExternalOutput").ap())
    gat_ggnn_kernel(nc, *args)
    r = _run(nc, [arrays], core_ids=[0])
    return r.results[0]["out_0_dram"]
```

```python
from contextlib import ExitStack

import concourse.bass as bass
from concourse import mybir

ALU = mybir.AluOpType
ACT = mybir.ActivationFunctionType
F32 = mybir.dt.float32
F32R = mybir.dt.float32r
I32 = mybir.dt.int32

P = 128
BANK = 512
STEPS = 5
EPS = 1e-5
NEG_BIG = 9000000000000000.0
SLOTS = 11264

Z, R, H = 0, 1, 2


def gat_ggnn_kernel(nc, x, adj, a, in_W, in_b, out_W, out_b, r_W, r_b, z_W, z_b, h_W, h_b,
                    o1_W, o1_b, o2_W, o2_b, out):
    N, DIM = x.shape
    assert DIM == 2 * P and N % 2 == 0
    NT = -(-N // P)
    LAST = N - (NT - 1) * P
    rows = [P] * (NT - 1) + [LAST]
    FT = NT - 1
    G3 = 3 * DIM
    TPC = BANK // P
    starts = list(range(0, N, BANK))
    chunks = [(c0, min(BANK, N - c0)) for c0 in starts]
    NC = len(chunks)
    LC = NC - 1
    assert NC == 3
    chunk_tiles = [[t for t in range(NT) if t * P // BANK == c] for c in range(NC)]
    early_tiles = [t for t in range(NT) if t * P // BANK < LC]
    late_tiles = chunk_tiles[LC]

    x1_dram = nc.dram_tensor("x1_scratch", (N, DIM), F32).ap()

    ctx = ExitStack()
    with ctx:
        base = -(-nc.sbuf_base // 32) * 32

        def place(name, shape, dtype, offset):
            words = 1
            for n in shape[1:]:
                words *= n
            offset += offset % 8
            assert base + offset + 4 * words <= nc.sbuf_usable_end, (name, offset)
            return nc.alloc_sbuf_tensor_at(name, shape, dtype, offset=base + offset, align_bytes=8), \
                offset + 4 * words

        A_rows, at = place("A_rows", [P, NT, N], F32R, 0)
        cols_at = at
        A_cols, at = place("A_cols", [P, NT, N], F32R, at)
        ident, at = place("ident", [P, P], F32, at)
        beta, at = place("beta", [P, 2, 6], F32, at)
        gate_b, at = place("gate_b", [P, 6], F32, at)
        arena = at
        W_hi, at = place("W_hi", [P, 6, G3], F32R, arena)
        W_lo, at = place("W_lo", [P, 6, G3], F32R, at)
        nodes_at = at
        S_hi, lo_at = place("S_hi", [P, NT, DIM], F32R, nodes_at)
        S_lo, at = place("S_lo", [P, NT, DIM], F32R, lo_at)
        ST, at = place("ST", [P, 2, N], F32, at)
        uv_at = at
        UV_hi, at = place("UV_hi", [P, 4, BANK], F32R, at)
        UV_lo, at = place("UV_lo", [P, 4, BANK], F32R, at)
        SC_hi, at = place("SC_hi", [P, 2, BANK], F32R, at)
        SC_lo, at = place("SC_lo", [P, 2, BANK], F32R, at)
        tmp, at = place("tmp", [P, BANK], F32, at)
        degree_at = at
        DEG, at = place("DEG", [P, 2, N], F32, at)
        A_int, at = place("A_int", [P, 2, N], I32, arena)
        scores, at = place("scores", [P, 2, N], F32, at)
        leaky, at = place("leaky", [P, 1, N], F32, at)
        b_row, at = place("b_row", [P, N], F32, at)
        A_sum, at = place("A_sum", [P, N], F32, nodes_at + 2 * NT * DIM * 4)
        PT, at = place("PT", [P, 2, NT, P], F32, nodes_at)
        h, at = place("h", [P, NT, DIM], F32, lo_at)
        product, at = place("product", [P, NT, DIM], F32, nodes_at)
        W_f32, at = place("W_f32", [P, 6, G3], F32, uv_at)
        X, at = place("X", [P, NT, DIM], F32, at)
        assert at <= degree_at + 4 * N
        at = nodes_at + 2 * NT * DIM * 4 + 4 * N
        stats, at = place("stats", [P, NT, 6], F32, at)
        mean_var, at = place("mean_var", [P, NT, 2], F32, at)
        std, at = place("std", [P, NT], F32, at)
        rstd, at = place("rstd", [P, NT], F32, at)
        newton, at = place("newton", [P, NT], F32, at)
        a_col, at = place("a_col", [P, NT], F32, at)
        b_col, at = place("b_col", [P, NT], F32, at)
        row_max, at = place("row_max", [P, NT], F32, at)
        neg_max, at = place("neg_max", [P, NT], F32, at)
        row_sum, at = place("row_sum", [P, NT], F32, at)
        inv_sum, at = place("inv_sum", [P, NT], F32, at)
        ones, at = place("ones", [P, P], F32R, at)
        assert at <= uv_at
        gate_nat, at = place("gate_nat", [P, 3, 2, G3], F32, cols_at)
        gate_T, at = place("gate_T", [P, 4, G3], F32, at)
        msg_nat, at = place("msg_nat", [P, 2, 2, DIM], F32, at)
        msg_bias, at = place("msg_bias", [P, 2, 2], F32, at)
        a_bc, at = place("a_bc", [P, 2, DIM], F32, at)
        assert at <= 2 * cols_at
        o_nat, at = place("o_nat", [P, 2, 2, DIM], F32, 0)
        o_T, at = place("o_T", [P, 2, 2, DIM], F32, at)
        o1_bias, at = place("o1_bias", [P, 2], F32, at)
        o2_bias, at = place("o2_bias", [P, DIM], F32, at)
        x1_back, at = place("x1_back", [P, NT, DIM], F32, at)
        result, at = place("result", [P, NT, DIM], F32, at)
        assert at <= cols_at
        YT, at = place("YT", [P, 2, N], F32, cols_at)

        def f32(ap):
            return ap.bitcast(F32)

        uvp = ctx.enter_context(nc.psum_tensor("uvp", [P, 4, BANK], F32))
        gp = ctx.enter_context(nc.psum_tensor("gp", [P, 4, BANK], F32))

        def sem(name):
            return ctx.enter_context(nc.semaphore(name))

        a_in, msg_in, bias_in = sem("a_in"), sem("msg_in"), sem("bias_in")
        x_in = [sem(f"x_in{q}") for q in range(NC)]
        gate_in = [sem(f"gate_in{g}") for g in range(3)]
        adj_in = [sem("adj_in_even"), sem("adj_in_odd")]
        x1_out, o_in, x1_in, result_out = sem("x1_out"), sem("o_in"), sem("x1_in"), sem("result_out")
        ident_ready = sem("ident_ready")
        var_ready, std_ready = sem("var_ready"), sem("std_ready")
        b_ready, b_full, b_copied, a_ready = sem("b_ready"), sem("b_full"), sem("b_copied"), sem("a_ready")
        wt_full, wt_copied = sem("wt_full"), sem("wt_copied")
        fused_full, fused_copied = sem("fused_full"), sem("fused_copied")
        beta_full, beta_ready = sem("beta_full"), sem("beta_ready")
        converted, summed = sem("converted"), sem("summed")
        at_full, at_copied = sem("at_full"), sem("at_copied")
        leaky_ready, score_ready, prob_ready = sem("leaky_ready"), sem("score_ready"), sem("prob_ready")
        pt_full, pt_copied = sem("pt_full"), sem("pt_copied")
        att_full, x1_ready = sem("att_full"), sem("x1_ready")
        w_hi_ready, w_ready = sem("w_hi_ready"), sem("w_ready")
        ln2_ready, ln2_T_full, st_ready = (sem(n) for n in
                                                        ("ln2_ready", "ln2_T_full", "st_ready"))
        degree_full, degree_ready = sem("degree_full"), sem("degree_ready")
        uv_full, uv_hi, uv_ready = sem("uv_full"), sem("uv_hi"), sem("uv_ready")
        sc_ready = sem("sc_ready")
        r_full, r_sum, r_act, r_used, rs_ready = (sem(n) for n in
                                                  ("r_full", "r_sum", "r_act", "r_used", "rs_ready"))
        z_full, z_sum, z_act = sem("z_full"), sem("z_sum"), sem("z_act")
        h_full, h_sum, h_act = sem("h_full"), sem("h_sum"), sem("h_act")
        updated = sem("updated")
        t_full, t_hi, t_ready = sem("t_full"), sem("t_hi"), sem("t_ready")
        oT_full, oT_copied, y_full, y_ready = sem("oT_full"), sem("oT_copied"), sem("y_full"), sem("y_ready")
        r_out_full, x1b_ready, result_ready = sem("r_out_full"), sem("x1b_ready"), sem("result_ready")
        dve_done, loop_done = sem("dve_done"), sem("loop_done")
        pool_done = sem("pool_done")

        ln2_banks = [uvp[:, 0, :], uvp[:, 1, :], uvp[:, 2, :], uvp[:, 3, :], gp[:, 3, :], uvp[:, 0, :]]
        fills = [list(range(q, min(q + TPC, NT))) for q in range(0, NT, TPC)]
        NF = len(fills)

        block = ctx.enter_context(nc.Block())

        @block.sync
        def _(sp):
            for q in range(NC):
                t0, t1 = chunk_tiles[q][0], min(chunk_tiles[q][-1] + 1, FT)
                sp.dma_start(X[:, t0:t1, :],
                             x[t0 * P:t1 * P, :].rearrange("(t p) d -> p t d", p=P)).then_inc(x_in[q], 16)
            sp.dma_start(X[0:LAST, FT, :], x[FT * P:N, :]).then_inc(x_in[LC], 16)
            sp.dma_start(a_bc[:, :, :].rearrange("p k d -> p (k d)"),
                         a.rearrange("k o -> o k").to_broadcast([P, 2 * DIM])).then_inc(a_in, 16)
            for g, w in ((Z, z_W), (R, r_W), (H, h_W)):
                sp.dma_start(gate_nat[:, g, :, :], w.rearrange("(c p) k -> p c k", p=P)).then_inc(gate_in[g], 16)
            for k, w in enumerate((in_W, out_W)):
                sp.dma_start(msg_nat[:, k, :, :], w.rearrange("(c p) k -> p c k", p=P)).then_inc(msg_in, 16)
            with nc.allow_non_contiguous_dma(reason="256 biases, one to a partition"):
                for k, b in enumerate((in_b, out_b)):
                    sp.dma_start(msg_bias[:, k, :], b.rearrange("(c p) -> p c", p=P)).then_inc(bias_in, 16)
                for g, b in ((Z, z_b), (R, r_b), (H, h_b)):
                    sp.dma_start(gate_b[:, 2 * g:2 * g + 2], b.rearrange("(c p) -> p c", p=P)).then_inc(bias_in, 16)
            for t in range(NT):
                if t >= 2:
                    sp.wait_ge(converted, t - 1)
                sp.dma_start(A_int[0:rows[t], t % 2, :],
                             adj[t * P:t * P + rows[t], :]).then_inc(adj_in[t % 2], 16)
            for t in range(NT):
                sp.wait_ge(x1_ready, t + 1)
                sp.dma_start(x1_dram[t * P:t * P + rows[t], :], X[0:rows[t], t, :]).then_inc(x1_out, 16)
            sp.wait_ge(uv_full, 4 * NC * STEPS)
            for k, w in enumerate((o1_W, o2_W)):
                sp.dma_start(o_nat[:, k, :, :], w.rearrange("(c p) k -> p c k", p=P)).then_inc(o_in, 16)
            with nc.allow_non_contiguous_dma(reason="256 biases, one to a partition"):
                sp.dma_start(o1_bias[:, :], o1_b.rearrange("(c p) -> p c", p=P)).then_inc(o_in, 16)
            sp.dma_start(o2_bias[:, :], o2_b.rearrange("(o m) -> o m", o=1).to_broadcast([P, DIM])).then_inc(x1_in, 16)
            sp.dma_start(x1_back[:, 0:FT, :], x1_dram[0:FT * P, :].rearrange("(t p) d -> p t d", p=P)).then_inc(x1_in, 16)
            sp.dma_start(x1_back[0:LAST, FT, :], x1_dram[FT * P:N, :]).then_inc(x1_in, 16)
            n = 0
            for t in range(0, NT, 2):
                n += 1
                sp.wait_ge(result_ready, min(t + 2, NT))
                if t + 1 < FT:
                    sp.dma_start(out[t * P:(t + 2) * P, :].rearrange("(t p) d -> p t d", p=P),
                                 result[:, t:t + 2, :]).then_inc(result_out, 16)
                else:
                    sp.dma_start(out[t * P:t * P + rows[t], :], result[0:rows[t], t, :]).then_inc(result_out, 16)
                    if t + 1 < NT:
                        n += 1
                        sp.dma_start(out[FT * P:N, :], result[0:LAST, FT, :]).then_inc(result_out, 16)
            sp.wait_ge(result_out, 16 * n)
            sp.wait_ge(x1_out, 16 * NT)

        @block.gpsimd
        def _(pool):
            pool.memset(ident[:, :], 0.0).then_inc(pool_done, 1)
            pool.wait_ge(pool_done, 1)
            pool.affine_select(out=ident[:, :], in_=ident[:, :], compare_op=ALU.not_equal, fill=1.0,
                               base=0, pattern=[[-1, P]], channel_multiplier=1).then_inc(ident_ready, 1)
            pool.memset(f32(ones[:, :]), 1.0).then_inc(ident_ready, 1)
            for t in range(NT):
                p = rows[t]
                pool.wait_ge(converted, t + 1)
                src = f32(A_rows[0:p, t, :])
                if t == 0:
                    pool.tensor_copy(A_sum[0:p, :], src).then_inc(summed, 1)
                else:
                    pool.wait_ge(summed, t)
                    pool.tensor_tensor(A_sum[0:p, :], A_sum[0:p, :], src, ALU.add).then_inc(summed, 1)

        @block.scalar
        def _(act):
            act.wait_ge(var_ready, 1)
            act.activation(std[:, :], mean_var[:, :, 1], ACT.Sqrt).then_inc(std_ready, 1)
            for f in range(9):
                g, pair = divmod(f, 3)
                act.wait_ge(wt_full, f + 1)
                dst = gate_T if pair < 2 else W_f32
                kk = 2 * pair if pair < 2 else 4
                act.activation(dst[:, kk:kk + 2, g * DIM:(g + 1) * DIM],
                               gp[:, f % 4, :].rearrange("p (k m) -> p k m", k=2), ACT.Copy).then_inc(wt_copied, 1)
            for q, tiles in enumerate(fills):
                n = min(N, (tiles[-1] + 1) * P) - tiles[0] * P
                act.wait_ge(b_full, q + 1)
                act.activation(b_row[:, tiles[0] * P:tiles[0] * P + n], uvp[:, q, 0:n], ACT.Copy).then_inc(b_copied, 1)
            for kt in range(4):
                act.wait_ge(fused_full, 2 * kt + 1)
                act.activation(W_f32[:, kt, 0:BANK], uvp[:, kt, :], ACT.Copy).then_inc(fused_copied, 1)
                act.wait_ge(fused_full, 2 * kt + 2)
                act.activation(W_f32[:, kt, BANK:G3], gp[:, kt, 0:G3 - BANK], ACT.Copy).then_inc(fused_copied, 1)
            act.wait_ge(beta_full, 1)
            act.activation(beta[:, :, :].rearrange("p k m -> p (k m)"), uvp[:, 3, 0:12], ACT.Copy).then_inc(beta_ready, 1)

            def columns(t):
                p = rows[t]
                for q, tiles in enumerate(fills):
                    act.wait_ge(at_full, NF * t + q + 1)
                    full = [k for k in tiles if k < FT]
                    last = act.activation(A_cols[:, full[0]:full[-1] + 1, t * P:t * P + p],
                                          gp[:, q, 0:len(full) * P].rearrange("p (k i) -> p k i", i=P)[:, :, 0:p],
                                          ACT.Copy)
                    if FT in tiles:
                        last = act.activation(A_cols[0:LAST, FT, t * P:t * P + p],
                                              gp[0:LAST, q, (FT - tiles[0]) * P:(FT - tiles[0]) * P + p],
                                              ACT.Copy)
                    last.then_inc(at_copied, 1)

            def leaky_scores(t):
                if t >= 1:
                    act.wait_ge(score_ready, t)
                act.activation(leaky[0:rows[t], 0, :], b_row[0:rows[t], :], ACT.Identity,
                               bias=a_col[0:rows[t], t:t + 1]).then_inc(leaky_ready, 1)

            act.wait_ge(b_copied, NF)
            act.wait_ge(a_ready, 1)
            leaky_scores(0)
            columns(0)
            columns(1)
            for t in range(NT):
                p = rows[t]
                if t + 1 < NT:
                    leaky_scores(t + 1)
                act.wait_ge(score_ready, t + 1)
                act.activation(scores[0:p, t % 2, :], scores[0:p, t % 2, :], ACT.Exp,
                               bias=neg_max[0:p, t:t + 1],
                               accum_out=row_sum[0:p, t:t + 1]).then_inc(prob_ready, 1)
                if t >= 2:
                    act.wait_ge(att_full, t - 1)
                for q, tiles in enumerate(fills):
                    act.wait_ge(pt_full, NF * t + q + 1)
                    full = [k for k in tiles if k < FT]
                    last = act.activation(PT[:, t % 2, full[0]:full[-1] + 1, 0:p],
                                          uvp[:, q, 0:len(full) * P].rearrange("p (k i) -> p k i", i=P)[:, :, 0:p],
                                          ACT.Copy)
                    if FT in tiles:
                        last = act.activation(PT[0:LAST, t % 2, FT, 0:p],
                                              uvp[0:LAST, q, (FT - tiles[0]) * P:(FT - tiles[0]) * P + p],
                                              ACT.Copy)
                    last.then_inc(pt_copied, 1)
                if t + 2 < NT:
                    columns(t + 2)
            act.wait_ge(pt_full, NF * NT)
            act.wait_ge(score_ready, NT)
            for g in range(3):
                act.activation(W_hi[:, :, g * DIM:(g + 1) * DIM], W_f32[:, :, g * DIM:(g + 1) * DIM],
                               ACT.Copy).then_inc(w_hi_ready, 1)
            act.wait_ge(var_ready, 2)
            act.activation(std[:, :], mean_var[:, :, 1], ACT.Sqrt).then_inc(std_ready, 1)
            for c, (c0, n) in enumerate(chunks):
                act.wait_ge(degree_full, c + 1)
                act.activation(DEG[:, 1, c0:c0 + n], gp[:, c, 0:n], ACT.Copy).then_inc(degree_ready, 1)
            act.wait_ge(degree_full, 2 * NC)
            for f in range(2 * NC):
                c, m = divmod(f, 2)
                c0, n = chunks[c]
                bank = ln2_banks[f][:, 0:n]
                act.wait_ge(ln2_T_full, f + 1)
                act.activation(ST[:, m, c0:c0 + n], bank, ACT.Relu).then_inc(st_ready, 1)
            act.wait_ge(w_ready, 3)
            act.wait_ge(x1_out, 16 * NT)
            for c, (c0, n) in enumerate(chunks):
                act.activation(DEG[:, 0, c0:c0 + n], gp[:, c, 0:n], ACT.Copy).then_inc(degree_ready, 1)

            with act.Fori(0, STEPS) as step:
                def state_hi(k, bank, t0, count, p):
                    act.wait_ge(t_full, step * 6 + k + 1)
                    act.activation(S_hi[0:p, t0:t0 + count, :],
                                   bank[0:p, 0:count * DIM].rearrange("p (t d) -> p t d", d=DIM),
                                   ACT.Copy).then_inc(t_hi, 1)

                state_hi(0, gp[:, 2, :], late_tiles[0], len(late_tiles) - 1, P)
                state_hi(1, gp[:, 3, :], FT, 1, LAST)
                for c, (c0, n) in enumerate(chunks):
                    for b in range(4):
                        act.wait_ge(uv_full, step * 12 + 4 * c + b + 1)
                        act.activation(UV_hi[:, b, 0:n], uvp[:, b, 0:n], ACT.Copy).then_inc(uv_hi, 1)
                    for m in range(2):
                        act.wait_ge(r_sum, step * 6 + 2 * c + m + 1)
                        act.activation(gp[:, m, 0:n], gp[:, m, 0:n], ACT.Sigmoid,
                                       bias=gate_b[:, 2 * R + m:2 * R + m + 1]).then_inc(r_act, 1)
                    if c == LC:
                        for k in range(4):
                            state_hi(2 + k, uvp[:, k, :], 2 * k, 2, P)
                    for m in range(2):
                        act.wait_ge(z_sum, step * 6 + 2 * c + m + 1)
                        act.activation(gp[:, 2 + m, 0:n], gp[:, 2 + m, 0:n], ACT.Sigmoid,
                                       bias=gate_b[:, 2 * Z + m:2 * Z + m + 1]).then_inc(z_act, 1)
                    for m in range(2):
                        act.wait_ge(h_sum, step * 6 + 2 * c + m + 1)
                        act.activation(gp[:, m, 0:n], gp[:, m, 0:n], ACT.Tanh,
                                       bias=gate_b[:, 2 * H + m:2 * H + m + 1]).then_inc(h_act, 1)

            for k in range(2):
                act.wait_ge(oT_full, k + 1)
                act.activation(o_T[:, k, :, :], uvp[:, k, :].rearrange("p (c m) -> p c m", c=2),
                               ACT.Copy).then_inc(oT_copied, 1)
            for f in range(2 * NC):
                c, m = divmod(f, 2)
                c0, n = chunks[c]
                act.wait_ge(y_full, f + 1)
                act.activation(YT[:, m, c0:c0 + n], gp[:, f % 4, 0:n], ACT.Tanh,
                               bias=o1_bias[:, m:m + 1]).then_inc(y_ready, 1)

        @block.vector
        def _(dve):
            chain = [0]

            def then(instruction):
                chain[0] += 1
                instruction.then_inc(dve_done, 1)
                dve.wait_ge(dve_done, chain[0])

            def statistics(tiles):
                for t in tiles:
                    last = dve.bn_stats(stats[0:rows[t], t, :], X[0:rows[t], t, :])
                then(last)
                for t in tiles:
                    last = dve.bn_aggr(mean_var[0:rows[t], t, :], stats[0:rows[t], t, :])
                return last

            def reciprocal_deviation(turn):
                dve.tensor_scalar(mean_var[:, :, 1], mean_var[:, :, 1], EPS, None, ALU.add).then_inc(var_ready, 1)
                dve.wait_ge(std_ready, turn)
                then(dve.reciprocal(rstd[:, :], std[:, :]))
                then(dve.tensor_tensor(newton[:, :], rstd[:, :], rstd[:, :], ALU.mult))
                then(dve.tensor_tensor(newton[:, :], newton[:, :], mean_var[:, :, 1], ALU.mult))
                then(dve.tensor_scalar(newton[:, :], newton[:, :], -0.5, 1.5, ALU.mult, ALU.add))
                then(dve.tensor_tensor(rstd[:, :], rstd[:, :], newton[:, :], ALU.mult))

            def normalise(t):
                p = rows[t]
                return dve.tensor_scalar(h[0:p, t, :], X[0:p, t, :], mean_var[0:p, t, 0:1], rstd[0:p, t:t + 1],
                                         ALU.subtract, ALU.mult)

            then(dve.memset(mean_var[:, :, :], 1.0))
            for q, tiles in enumerate(chunk_tiles):
                dve.wait_ge(x_in[q], 32 if q == LC else 16)
                last = statistics(tiles)
            then(last)
            reciprocal_deviation(1)
            for t in range(NT):
                last = normalise(t)
            then(last)
            dve.tensor_scalar(h[:, 0:FT, :], h[:, 0:FT, :], 0.0, None, ALU.max)
            then(dve.tensor_scalar(h[0:LAST, FT, :], h[0:LAST, FT, :], 0.0, None, ALU.max))
            def convert(t):
                p = rows[t]
                dve.wait_ge(adj_in[t % 2], 16 * (t // 2 + 1))
                dve.tensor_copy(A_rows[0:p, t, :], A_int[0:p, t % 2, :]).then_inc(converted, 1)

            dve.wait_ge(a_in, 16)
            for half, col, ready in ((1, b_col, b_ready), (0, a_col, a_ready)):
                for t in range(NT):
                    p = rows[t]
                    last = dve.tensor_tensor_reduce(product[0:p, t, :], h[0:p, t, :], a_bc[0:p, half, :], 1.0, 0.0,
                                                    ALU.mult, ALU.add, col[0:p, t:t + 1])
                last.then_inc(ready, 1)
                dve.wait_ge(ready, 1)

            convert(0)
            convert(1)

            def score(t):
                p = rows[t]
                s = scores[0:p, t % 2, :]
                dve.wait_ge(converted, t + 1)
                if t >= 2:
                    dve.wait_ge(pt_full, NF * (t - 1))
                then(dve.tensor_scalar(s, f32(A_rows[0:p, t, :]), 0.0, NEG_BIG, ALU.is_le, ALU.mult))
                dve.wait_ge(leaky_ready, t + 1)
                then(dve.scalar_tensor_tensor(leaky[0:p, 0, :], leaky[0:p, 0, :], 0.01, leaky[0:p, 0, :],
                                              ALU.mult, ALU.max))
                then(dve.tensor_tensor_reduce(s, leaky[0:p, 0, :], s, 1.0, -3.0e38,
                                              ALU.subtract, ALU.max, row_max[0:p, t:t + 1]))
                dve.tensor_scalar(neg_max[0:p, t:t + 1], row_max[0:p, t:t + 1], -1.0, None,
                                  ALU.mult).then_inc(score_ready, 1)

            def residual(t):
                p = rows[t]
                bank = uvp[0:p, 3, 0:DIM] if t % 2 == 0 else gp[0:p, 3, 0:DIM]
                dve.wait_ge(prob_ready, t + 1)
                then(dve.reciprocal(inv_sum[0:p, t:t + 1], row_sum[0:p, t:t + 1]))
                dve.wait_ge(att_full, t + 1)
                last = dve.scalar_tensor_tensor(X[0:p, t, :], bank, inv_sum[0:p, t:t + 1], X[0:p, t, :],
                                                ALU.mult, ALU.add)
                last.then_inc(x1_ready, 1)
                dve.wait_ge(x1_ready, t + 1)
                return statistics([t])

            score(0)
            for t in range(NT):
                if t + 2 < NT:
                    convert(t + 2)
                if t + 1 < NT:
                    score(t + 1)
                if t >= 1:
                    residual(t - 1)
            then(residual(NT - 1))
            reciprocal_deviation(2)
            dve.wait_ge(att_full, NT)
            for t in range(NT):
                last = normalise(t)
            then(last)
            early = len(early_tiles)
            dve.tensor_scalar(S_hi[:, 0:early, :], h[:, 0:early, :], 0.0, None, ALU.max).then_inc(ln2_ready, 1)
            for g in range(3):
                cols = slice(g * DIM, (g + 1) * DIM)
                dve.wait_ge(w_hi_ready, g + 1)
                dve.tensor_tensor(W_lo[:, :, cols], W_f32[:, :, cols], f32(W_hi[:, :, cols]),
                                  ALU.subtract).then_inc(w_ready, 1)
            dve.wait_ge(ln2_T_full, 2 * NC)
            dve.wait_ge(ln2_ready, 1)
            dve.scalar_tensor_tensor(S_lo[:, 0:early, :], h[:, 0:early, :], 0.0, f32(S_hi[:, 0:early, :]),
                                     ALU.max, ALU.subtract).then_inc(t_ready, 1)
            dve.wait_ge(w_ready, 3)
            dve.wait_ge(x1_out, 16 * NT)
            dve.wait_ge(st_ready, 2 * NC)
            dve.memset(tmp[0:1, 0:2], 0.0).then_inc(updated, 1)

            with dve.Fori(0, STEPS) as step:
                links = [0]
                per_step = 13 * NC

                def link(instruction):
                    links[0] += 1
                    instruction.then_inc(loop_done, 1)
                    dve.wait_ge(loop_done, step * per_step + links[0])

                def split_chunk(c):
                    c0, n = chunks[c]
                    link(dve.tensor_copy(SC_hi[:, :, 0:n], ST[:, :, c0:c0 + n]))
                    dve.tensor_tensor(SC_lo[:, :, 0:n], ST[:, :, c0:c0 + n], f32(SC_hi[:, :, 0:n]),
                                      ALU.subtract).then_inc(sc_ready, 1)

                def state_lo(k, bank, t0, count, p):
                    dve.wait_ge(t_hi, step * 6 + k + 1)
                    dve.tensor_tensor(S_lo[0:p, t0:t0 + count, :],
                                      bank[0:p, 0:count * DIM].rearrange("p (t d) -> p t d", d=DIM),
                                      f32(S_hi[0:p, t0:t0 + count, :]), ALU.subtract).then_inc(t_ready, 1)

                def add_degrees(full, sums, g, b0, c):
                    c0, n = chunks[c]
                    for m in range(2):
                        bank = gp[:, b0 + m, 0:n]
                        dve.wait_ge(full, step * 6 + 2 * c + m + 1)
                        if c == 0 and g == R and m == 0:
                            dve.wait_ge(degree_ready, 2 * NC)
                        link(dve.scalar_tensor_tensor(bank, DEG[:, 1, c0:c0 + n], beta[:, 0, 2 * g + m:2 * g + m + 1],
                                                      bank, ALU.mult, ALU.add))
                        dve.scalar_tensor_tensor(bank, DEG[:, 0, c0:c0 + n], beta[:, 1, 2 * g + m:2 * g + m + 1],
                                                 bank, ALU.mult, ALU.add).then_inc(sums, 1)

                split_chunk(0)
                state_lo(0, gp[:, 2, :], late_tiles[0], len(late_tiles) - 1, P)
                state_lo(1, gp[:, 3, :], FT, 1, LAST)
                for c, (c0, n) in enumerate(chunks):
                    for b in range(4):
                        dve.wait_ge(uv_hi, step * 12 + 4 * c + b + 1)
                        dve.tensor_tensor(UV_lo[:, b, 0:n], uvp[:, b, 0:n], f32(UV_hi[:, b, 0:n]),
                                          ALU.subtract).then_inc(uv_ready, 1)
                    add_degrees(r_full, r_sum, R, 0, c)
                    for m in range(2):
                        dve.wait_ge(r_act, step * 6 + 2 * c + m + 1)
                        if m == 1:
                            dve.wait_ge(rs_ready, step * 6 + 2 * c + 1)
                        ins = dve.tensor_tensor(tmp[:, 0:n], gp[:, m, 0:n], ST[:, m, c0:c0 + n], ALU.mult)
                        ins.then_inc(r_used, 1)
                        dve.wait_ge(r_used, step * 6 + 2 * c + m + 1)
                        link(dve.tensor_copy(SC_hi[:, m, 0:n], tmp[:, 0:n]))
                        dve.tensor_tensor(SC_lo[:, m, 0:n], tmp[:, 0:n], f32(SC_hi[:, m, 0:n]),
                                          ALU.subtract).then_inc(rs_ready, 1)
                    if c == LC:
                        for k in range(4):
                            state_lo(2 + k, uvp[:, k, :], 2 * k, 2, P)
                    add_degrees(z_full, z_sum, Z, 2, c)
                    add_degrees(h_full, h_sum, H, 0, c)
                    for m in range(2):
                        dve.wait_ge(h_act, step * 6 + 2 * c + m + 1)
                        if m == 0:
                            dve.wait_ge(rs_ready, step * 6 + 2 * c + 2)
                        else:
                            dve.wait_ge(updated, step * 6 + 2 * c + 2)
                        link(dve.tensor_tensor(tmp[:, 0:n], gp[:, m, 0:n], ST[:, m, c0:c0 + n], ALU.subtract))
                        dve.wait_ge(z_act, step * 6 + 2 * c + m + 1)
                        link(dve.tensor_tensor(tmp[:, 0:n], gp[:, 2 + m, 0:n], tmp[:, 0:n], ALU.mult))
                        dve.tensor_tensor(ST[:, m, c0:c0 + n], ST[:, m, c0:c0 + n], tmp[:, 0:n],
                                          ALU.add).then_inc(updated, 1)
                    dve.wait_ge(updated, step * 6 + 2 * c + 3)
                    if c < LC:
                        split_chunk(c + 1)
                assert links[0] == per_step

            dve.wait_ge(x1_in, 48)
            for t in range(NT):
                p = rows[t]
                last = dve.tensor_tensor(x1_back[0:p, t, :], x1_back[0:p, t, :], o2_bias[0:p, :], ALU.add)
            last.then_inc(x1b_ready, 1)
            dve.wait_ge(x1b_ready, 1)
            for t in range(NT):
                p = rows[t]
                dve.wait_ge(r_out_full, t + 1)
                dve.tensor_tensor(result[0:p, t, :], uvp[0:p, t % 4, 0:DIM], x1_back[0:p, t, :],
                                  ALU.add).then_inc(result_ready, 1)

        @block.tensor
        def _(pe):
            pe.wait_ge(ident_ready, 2)
            for f in range(9):
                g, pair = divmod(f, 3)
                if pair == 0:
                    pe.wait_ge(gate_in[g], 16)
                if f >= 4:
                    pe.wait_ge(wt_copied, f - 3)
                for kk in range(2):
                    for m in range(2):
                        k0 = (2 * pair + kk) * P
                        last = pe.transpose(gp[:, f % 4, kk * DIM + m * P:kk * DIM + (m + 1) * P],
                                            gate_nat[:, g, m, k0:k0 + P], ident[:, :])
                last.then_inc(wt_full, 1)
            pe.wait_ge(b_ready, 1)
            for q, tiles in enumerate(fills):
                for t in tiles:
                    p = rows[t]
                    last = pe.matmul(uvp[:, q, (t - tiles[0]) * P:(t - tiles[0]) * P + p],
                                     b_col[0:p, t:t + 1].to_broadcast([p, P]), ident[0:p, 0:p],
                                     start=True, stop=True)
                last.then_inc(b_full, 1)

            pe.wait_ge(msg_in, 32)
            pe.wait_ge(wt_copied, 9)
            pe.wait_ge(b_copied, NF)
            for kt in range(4):
                k, half = divmod(kt, 2)
                for bank, c0, n in ((uvp, 0, BANK), (gp, BANK, G3 - BANK)):
                    for tt in range(2):
                        last = pe.matmul(bank[:, kt, 0:n], msg_nat[:, k, tt, half * P:(half + 1) * P],
                                         gate_T[:, 2 * k + tt, c0:c0 + n], start=(tt == 0), stop=(tt == 1))
                    last.then_inc(fused_full, 1)
            pe.wait_ge(bias_in, 16 * 5)
            pe.wait_ge(fused_copied, 8)
            for k in range(2):
                for mt in range(6):
                    for tt in range(2):
                        last = pe.matmul(uvp[:, 3, 6 * k + mt:6 * k + mt + 1],
                                         gate_T[:, 2 * k + tt, mt * P:(mt + 1) * P],
                                         msg_bias[:, k, tt:tt + 1], start=(tt == 0), stop=(tt == 1))
            last.then_inc(beta_full, 1)
            pe.wait_ge(beta_ready, 1)

            def transpose_adjacency(t):
                p = rows[t]
                pe.wait_ge(converted, t + 1)
                for q, tiles in enumerate(fills):
                    if t >= 1:
                        pe.wait_ge(at_copied, NF * (t - 1) + q + 1)
                    for k in tiles:
                        last = pe.transpose(gp[0:rows[k], q, (k - tiles[0]) * P:(k - tiles[0]) * P + p],
                                            f32(A_rows[0:p, t, k * P:k * P + rows[k]]), ident[0:p, 0:p])
                    last.then_inc(at_full, 1)

            transpose_adjacency(0)
            transpose_adjacency(1)
            for t in range(NT):
                p = rows[t]
                pe.wait_ge(prob_ready, t + 1)
                for q, tiles in enumerate(fills):
                    if t >= 1:
                        pe.wait_ge(pt_copied, NF * (t - 1) + q + 1)
                    for k in tiles:
                        last = pe.transpose(uvp[0:rows[k], q, (k - tiles[0]) * P:(k - tiles[0]) * P + p],
                                            scores[0:p, t % 2, k * P:k * P + rows[k]], ident[0:p, 0:p])
                    last.then_inc(pt_full, 1)
                if t + 2 < NT:
                    transpose_adjacency(t + 2)
                if t >= 2:
                    pe.wait_ge(x1_ready, t - 1)
                bank = uvp[0:p, 3, 0:DIM] if t % 2 == 0 else gp[0:p, 3, 0:DIM]
                for k in range(NT):
                    if k % TPC == 0:
                        pe.wait_ge(pt_copied, NF * t + k // TPC + 1)
                    last = pe.matmul(bank, PT[0:rows[k], t % 2, k, 0:p], h[0:rows[k], k, :],
                                     start=(k == 0), stop=(k == NT - 1))
                last.then_inc(att_full, 1)
            pe.wait_ge(at_copied, NF * NT)
            for c, (c0, n) in enumerate(chunks):
                for t in range(NT):
                    last = pe.matmul(gp[:, c, 0:n], ones[0:rows[t], :], A_cols[0:rows[t], t, c0:c0 + n],
                                     start=(t == 0), stop=(t == NT - 1))
                last.then_inc(degree_full, 1)
            pe.wait_ge(summed, NT)
            for c, (c0, n) in enumerate(chunks):
                pe.wait_ge(degree_ready, c + 1)
                pe.matmul(gp[:, c, 0:n], f32(ones[:, :]), A_sum[:, c0:c0 + n],
                          start=True, stop=True).then_inc(degree_full, 1)
            pe.wait_ge(ln2_ready, 1)
            for f in range(2 * NC):
                c, m = divmod(f, 2)
                bank = ln2_banks[f]
                if f == 0:
                    pe.wait_ge(x1_ready, NT)
                if f == 5:
                    pe.wait_ge(st_ready, 1)
                for t in chunk_tiles[c]:
                    p = rows[t]
                    i0 = t * P - chunks[c][0]
                    last = pe.transpose(bank[:, i0:i0 + p], h[0:p, t, m * P:(m + 1) * P], ident[0:p, 0:p])
                last.then_inc(ln2_T_full, 1)
            pe.wait_ge(st_ready, 2 * NC)

            with pe.Fori(0, STEPS) as step:
                def propagate(b, c, tiles, first, final):
                    c0, n = chunks[c]
                    m = b % 2
                    A = A_cols if b < 2 else A_rows
                    for t in tiles:
                        p = rows[t]
                        for part in (S_hi, S_lo):
                            ins = pe.matmul(uvp[:, b, 0:n], part[0:p, t, m * P:(m + 1) * P], A[0:p, t, c0:c0 + n],
                                            start=(first and t == tiles[0] and part is S_hi),
                                            stop=(final and t == tiles[-1] and part is S_lo))
                    if final:
                        ins.then_inc(uv_full, 1)

                def transpose_state(bank, tiles, column=0):
                    for i, t in enumerate(tiles):
                        p = rows[t]
                        for m in range(2):
                            ins = pe.transpose(bank[0:p, i * DIM + m * P:i * DIM + (m + 1) * P],
                                               ST[:, m, t * P:t * P + p], ident[:, :])
                    ins.then_inc(t_full, 1)

                def gate(bank, n, g, m, operands, first, final):
                    cols = slice(g * DIM + m * P, g * DIM + (m + 1) * P)
                    for i, (kt, hi, lo) in enumerate(operands):
                        for j, (w, v) in enumerate(((W_hi, hi), (W_hi, lo), (W_lo, hi))):
                            ins = pe.matmul(bank, w[:, kt, cols], v, start=(first and i == 0 and j == 0),
                                            stop=(final and i == len(operands) - 1 and j == 2))
                    return ins

                pe.wait_ge(t_ready, step * 6 + 1)
                for b in range(3):
                    propagate(b, 0, early_tiles, True, False)
                pe.wait_ge(updated, step * 6 + 1)
                pe.wait_ge(degree_ready, 2 * NC)
                transpose_state(gp[:, 2, :], late_tiles[:-1])
                transpose_state(gp[:, 3, :], late_tiles[-1:])
                propagate(3, 0, early_tiles, True, False)
                pe.wait_ge(t_ready, step * 6 + 3)
                for c, (c0, n) in enumerate(chunks):
                    for b in range(4):
                        if c == 0:
                            propagate(b, 0, late_tiles, False, True)
                        else:
                            pe.wait_ge(uv_ready, step * 12 + 4 * (c - 1) + b + 1)
                            propagate(b, c, list(range(NT)), True, True)
                    state = [(4 + k, SC_hi[:, k, 0:n], SC_lo[:, k, 0:n]) for k in range(2)]
                    message = [(k, UV_hi[:, k, 0:n], UV_lo[:, k, 0:n]) for k in range(4)]
                    pe.wait_ge(sc_ready, step * 3 + c + 1)
                    if c == 0:
                        pe.wait_ge(w_ready, 3)
                    if c > 0:
                        pe.wait_ge(updated, step * 6 + 2 * c + 1)
                    for g, b0 in ((R, 0), (Z, 2)):
                        for m in range(2):
                            gate(gp[:, b0 + m, 0:n], n, g, m, state, True, False)
                    pe.wait_ge(uv_ready, step * 12 + 4 * (c + 1))
                    for m in range(2):
                        gate(gp[:, m, 0:n], n, R, m, message, False, True).then_inc(r_full, 1)
                    if c == LC:
                        for k in range(4):
                            transpose_state(uvp[:, k, :], [2 * k, 2 * k + 1])
                    for m in range(2):
                        gate(gp[:, 2 + m, 0:n], n, Z, m, message, False, True).then_inc(z_full, 1)
                    for m in range(2):
                        pe.wait_ge(r_used, step * 6 + 2 * c + m + 1)
                        gate(gp[:, m, 0:n], n, H, m, message, True, False)
                    pe.wait_ge(rs_ready, step * 6 + 2 * c + 2)
                    for m in range(2):
                        gate(gp[:, m, 0:n], n, H, m, state, False, True).then_inc(h_full, 1)

            pe.wait_ge(o_in, 48)
            pe.wait_ge(t_ready, 6 * STEPS + 1)
            for k in range(2):
                for c in range(2):
                    for m in range(2):
                        last = pe.transpose(uvp[:, k, c * DIM + m * P:c * DIM + (m + 1) * P],
                                            o_nat[:, k, m, c * P:(c + 1) * P], ident[:, :])
                last.then_inc(oT_full, 1)
            pe.wait_ge(oT_copied, 2)
            pe.wait_ge(updated, 6 * STEPS + 1)
            for f in range(2 * NC):
                c, m = divmod(f, 2)
                c0, n = chunks[c]
                if f >= 4:
                    pe.wait_ge(y_ready, f - 3)
                for k in range(2):
                    last = pe.matmul(gp[:, f % 4, 0:n], o_T[:, 0, k, m * P:(m + 1) * P], ST[:, k, c0:c0 + n],
                                     start=(k == 0), stop=(k == 1))
                last.then_inc(y_full, 1)
            for t in range(NT):
                p = rows[t]
                pe.wait_ge(y_ready, 2 * (t * P // BANK) + 2)
                if t >= 4:
                    pe.wait_ge(result_ready, t - 3)
                for k in range(2):
                    last = pe.matmul(uvp[0:p, t % 4, 0:DIM], YT[:, k, t * P:t * P + p], o_T[:, 1, k, :],
                                     start=(k == 0), stop=(k == 1))
                last.then_inc(r_out_full, 1)


_INS = ['x', 'adj', 'L0_gnn_a', 'L1_gnn_in_W', 'L1_gnn_in_b', 'L1_gnn_out_W', 'L1_gnn_out_b', 'L1_gnn_r_W',
        'L1_gnn_r_b', 'L1_gnn_z_W', 'L1_gnn_z_b', 'L1_gnn_h_W', 'L1_gnn_h_b', 'L1_gnn_o1_W', 'L1_gnn_o1_b',
        'L1_gnn_o2_W', 'L1_gnn_o2_b']


def kernel(**inputs):
    import numpy as _np
    import concourse.bacc as _bacc
    from concourse import mybir as _mybir
    from concourse.bass_utils import run_bass_kernel_spmd as _run

    nc = _bacc.Bacc("TRN2", target_bir_lowering=False, num_devices=1, dynamic_dma_scratch_size=256)
    arrays, args = {}, []
    for name in _INS:
        a = _np.ascontiguousarray(inputs[name])
        arrays[f"in_{name}_dram"] = a
        args.append(nc.dram_tensor(f"in_{name}_dram", a.shape, _mybir.dt.from_np(a.dtype), kind="ExternalInput").ap())
    args.append(nc.dram_tensor("out_0_dram", inputs['x'].shape, _mybir.dt.float32, kind="ExternalOutput").ap())
    gat_ggnn_kernel(nc, *args)
    r = _run(nc, [arrays], core_ids=[0])
    return r.results[0]["out_0_dram"]
```

```python
from contextlib import ExitStack

import concourse.bass as bass
from concourse import mybir

ALU = mybir.AluOpType
ACT = mybir.ActivationFunctionType
F32 = mybir.dt.float32
F32R = mybir.dt.float32r

P = 128
BANK = 512
STEPS = 5
EPS = 1e-5
NEG_BIG = 9000000000000000.0

Z, R, H = 0, 1, 2


def gat_ggnn_kernel(nc, x, adj, a, in_W, in_b, out_W, out_b, r_W, r_b, z_W, z_b, h_W, h_b,
                    o1_W, o1_b, o2_W, o2_b, out):
    N, DIM = x.shape
    assert DIM == 2 * P and N % 2 == 0
    NT = -(-N // P)
    LAST = N - (NT - 1) * P
    rows = [P] * (NT - 1) + [LAST]
    FT = NT - 1
    G3 = 3 * DIM
    TPC = BANK // P
    starts = list(range(0, N, BANK))
    chunks = [(c0, min(BANK, N - c0)) for c0 in starts]
    NC = len(chunks)
    LC = NC - 1
    assert NC == 3
    chunk_tiles = [[t for t in range(NT) if t * P // BANK == c] for c in range(NC)]
    early_tiles = [t for t in range(NT) if t * P // BANK < LC]
    late_tiles = chunk_tiles[LC]

    x1_dram = nc.dram_tensor("x1_scratch", (N, DIM), F32).ap()
    oT_dram = nc.dram_tensor("oT_scratch", (P, 4 * DIM), F32).ap()

    ctx = ExitStack()
    with ctx:
        base = -(-nc.sbuf_base // 32) * 32

        def place(name, shape, dtype, offset):
            words = 1
            for n in shape[1:]:
                words *= n
            offset += offset % 8
            assert base + offset + 4 * words <= nc.sbuf_usable_end, (name, offset)
            return nc.alloc_sbuf_tensor_at(name, shape, dtype, offset=base + offset, align_bytes=8), \
                offset + 4 * words

        A_rows, at = place("A_rows", [P, NT, N], F32R, 0)
        cols_at = at
        A_cols, at = place("A_cols", [P, NT, N], F32R, at)
        ident_r, at = place("ident_r", [P, P], F32R, at)
        degree_col, at = place("degree_col", [P, NT], F32, at)
        ones, at = place("ones", [P, P], F32R, at)
        beta, at = place("beta", [P, 2, 6], F32, at)
        gate_b, at = place("gate_b", [P, 6], F32, at)
        arena = at
        W_hi, at = place("W_hi", [P, 6, G3], F32R, arena)
        W_lo, at = place("W_lo", [P, 6, G3], F32R, at)
        nodes_at = at
        S_hi, lo_at = place("S_hi", [P, NT, DIM], F32R, nodes_at)
        S_lo, at = place("S_lo", [P, NT, DIM], F32R, lo_at)
        ST, at = place("ST", [P, 2, N], F32, at)
        uv_at = at
        UV_hi, at = place("UV_hi", [P, 4, BANK], F32R, at)
        UV_lo, at = place("UV_lo", [P, 4, BANK], F32R, at)
        SC_hi, at = place("SC_hi", [P, 2, BANK], F32R, at)
        SC_lo, at = place("SC_lo", [P, 2, BANK], F32R, at)
        tmp, at = place("tmp", [P, BANK], F32, at)
        degree_at = at
        DEG, at = place("DEG", [P, 2, N], F32, at)
        scores, at = place("scores", [P, 2, N], F32, arena)
        leaky_even, at = place("leaky_even", [P, N], F32, at)
        b_row, at = place("b_row", [P, N], F32, at)
        row_copy, _ = place("row_copy", [P, N], F32, at)
        centred, at = place("centred", [P, NT, DIM], F32, at)
        assert at <= nodes_at
        PT, at = place("PT", [P, 2, NT, P], F32, nodes_at)
        h, at = place("h", [P, NT, DIM], F32, lo_at)
        product, at = place("product", [P, NT, DIM], F32, nodes_at)
        W_f32, at = place("W_f32", [P, 6, G3], F32, uv_at)
        X, at = place("X", [P, NT, DIM], F32, at)
        assert at <= degree_at + 4 * N
        leaky_odd, at = place("leaky_odd", [P, N], F32, degree_at + 4 * N)
        leaky = [leaky_even, leaky_odd]
        oT_out, _ = place("oT_out", [P, 2, 2, DIM], F32, lo_at + NT * DIM * 4)
        at = uv_at - 4 * chunks[LC][1]
        stats, at = place("stats", [P, NT, 6], F32, at)
        mean_var, at = place("mean_var", [P, NT, 2], F32, at)
        std, at = place("std", [P, NT], F32, at)
        neg_mean, at = place("neg_mean", [P, NT], F32, at)
        rstd, at = place("rstd", [P, NT], F32, at)
        newton, at = place("newton", [P, NT], F32, at)
        a_col, at = place("a_col", [P, NT], F32, at)
        b_col, at = place("b_col", [P, NT], F32, at)
        row_max, at = place("row_max", [P, NT], F32, at)
        neg_max, at = place("neg_max", [P, NT], F32, at)
        row_sum, at = place("row_sum", [P, NT], F32, at)
        warm, at = place("warm", [P, 2], F32, at)
        inv_sum, at = place("inv_sum", [P, NT], F32, at)
        assert at <= uv_at
        gate_nat, at = place("gate_nat", [P, 3, 2, G3], F32, cols_at)
        gate_T, at = place("gate_T", [P, 4, G3], F32, at)
        msg_nat, at = place("msg_nat", [P, 2, 2, DIM], F32, at)
        msg_bias, at = place("msg_bias", [P, 2, DIM], F32, at)
        bias_product, at = place("bias_product", [P, 12, DIM], F32, at)
        a_bc, at = place("a_bc", [P, 2, DIM], F32, at)
        o_nat, at = place("o_nat", [P, 2, 2, DIM], F32, at)
        assert at <= 2 * cols_at
        o_T, at = place("o_T", [P, 2, 2, DIM], F32, 0)
        o1_bias, at = place("o1_bias", [P, 2], F32, at)
        o2_bias, at = place("o2_bias", [P, DIM], F32, at)
        x1_back, at = place("x1_back", [P, NT, DIM], F32, at)
        result, at = place("result", [P, NT, DIM], F32, at)
        assert at <= cols_at
        YT, at = place("YT", [P, 2, N], F32, cols_at)

        def f32(ap):
            return ap.bitcast(F32)

        ident = f32(ident_r[:, :])

        uvp = ctx.enter_context(nc.psum_tensor("uvp", [P, 4, BANK], F32))
        gp = ctx.enter_context(nc.psum_tensor("gp", [P, 4, BANK], F32))

        def sem(name):
            return ctx.enter_context(nc.semaphore(name))

        a_in, msg_in, bias_in, gate_b_in = sem("a_in"), sem("msg_in"), sem("bias_in"), sem("gate_b_in")
        x_in = [sem(f"x_in{q}") for q in range(NC)]
        gate_in = [sem(f"gate_in{g}") for g in range(3)]
        adj_in = [sem(f"adj_in{t}") for t in range(NT)]
        o_nat_in, oT_stored = sem("o_nat_in"), sem("oT_stored")
        x1_out, o_in, x1_in, result_out = sem("x1_out"), sem("o_in"), sem("x1_in"), sem("result_out")
        ident_ready = sem("ident_ready")
        var_ready, std_ready = sem("var_ready"), sem("std_ready")
        mean_ready, centred_ready = sem("mean_ready"), sem("centred_ready")
        b_ready, b_full, b_copied, a_ready = sem("b_ready"), sem("b_full"), sem("b_copied"), sem("a_ready")
        wt_full, wt_copied = sem("wt_full"), sem("wt_copied")
        fused_full, fused_copied = sem("fused_full"), sem("fused_copied")
        beta_ready, h_ready, late_h_ready = sem("beta_ready"), sem("h_ready"), sem("late_h_ready")
        row_summed, row_summed_odd = sem("row_summed"), sem("row_summed_odd")
        at_full, at_copied = sem("at_full"), sem("at_copied")
        leaky_ready, score_ready, prob_ready = sem("leaky_ready"), sem("score_ready"), sem("prob_ready")
        pt_full, pt_copied = sem("pt_full"), sem("pt_copied")
        att_full, x1_ready = sem("att_full"), sem("x1_ready")
        w_hi_ready, w_ready = sem("w_hi_ready"), sem("w_ready")
        ln2_ready, ln2_T_full, st_ready = sem("ln2_ready"), sem("ln2_T_full"), sem("st_ready")
        degree_full, degree_ready = sem("degree_full"), sem("degree_ready")
        uv_full, uv_hi, uv_ready = sem("uv_full"), sem("uv_hi"), sem("uv_ready")
        sc_ready = sem("sc_ready")
        r_full, r_sum, r_act, r_used, rs_ready = (sem(n) for n in
                                                  ("r_full", "r_sum", "r_act", "r_used", "rs_ready"))
        z_full, z_sum, z_act = sem("z_full"), sem("z_sum"), sem("z_act")
        h_full, h_sum, h_act = sem("h_full"), sem("h_sum"), sem("h_act")
        updated = sem("updated")
        t_full, t_hi, t_ready = sem("t_full"), sem("t_hi"), sem("t_ready")
        oT_full, oT_copied, y_full, y_ready = sem("oT_full"), sem("oT_copied"), sem("y_full"), sem("y_ready")
        r_out_full, x1b_ready, result_ready = sem("r_out_full"), sem("x1b_ready"), sem("result_ready")
        dve_done, loop_done = sem("dve_done"), sem("loop_done")
        pool_done = sem("pool_done")

        b_banks = [uvp[:, 2, :], uvp[:, 3, :], gp[:, 1, :]]
        y_banks = [uvp[:, 2, :], uvp[:, 3, :], uvp[:, 0, :], uvp[:, 1, :], gp[:, 0, :], gp[:, 1, :]]
        out_banks = [gp[:, 2, :], gp[:, 3, :], uvp[:, 2, :], uvp[:, 3, :]]
        ln2_banks = [gp[:, 0, :], gp[:, 1, :], gp[:, 2, :], uvp[:, 3, :], gp[:, 3, :], uvp[:, 0, :]]
        fills = [list(range(q, min(q + TPC, NT))) for q in range(0, NT, TPC)]
        NF = len(fills)
        H_SPLIT = 3

        block = ctx.enter_context(nc.Block())

        @block.sync
        def _(sp):
            gates = ((Z, z_W, z_b), (R, r_W, r_b), (H, h_W, h_b))
            for q in range(NC):
                t0, t1 = chunk_tiles[q][0], min(chunk_tiles[q][-1] + 1, FT)
                sp.dma_start(X[:, t0:t1, :],
                             x[t0 * P:t1 * P, :].rearrange("(t p) d -> p t d", p=P)).then_inc(x_in[q], 16)
                if q == 0:
                    sp.dma_start(a_bc[:, :, :].rearrange("p k d -> p (k d)"),
                                 a.rearrange("k o -> o k").to_broadcast([P, 2 * DIM])).then_inc(a_in, 16)
                if q == LC:
                    sp.dma_start(X[0:LAST, FT, :], x[FT * P:N, :]).then_inc(x_in[LC], 16)
                    for k, w in enumerate((in_W, out_W)):
                        sp.dma_start(msg_nat[:, k, :, :], w.rearrange("(c p) k -> p c k", p=P)).then_inc(msg_in, 16)
                if q == 1:
                    for k, b in enumerate((in_b, out_b)):
                        sp.dma_start(msg_bias[:, k, :], b.rearrange("(o m) -> o m", o=1).to_broadcast([P, DIM])).then_inc(bias_in, 16)
                g, w, _ = gates[q]
                sp.dma_start(gate_nat[:, g, :, :], w.rearrange("(c p) k -> p c k", p=P)).then_inc(gate_in[g], 16)
            with nc.allow_non_contiguous_dma(reason="256 biases, one to a partition"):
                for g, _, b in gates:
                    sp.dma_start(gate_b[:, 2 * g:2 * g + 2], b.rearrange("(c p) -> p c", p=P)).then_inc(gate_b_in, 16)
            for k, w in enumerate((o1_W, o2_W)):
                sp.dma_start(o_nat[:, k, :, :], w.rearrange("(c p) k -> p c k", p=P)).then_inc(o_nat_in, 16)
            sp.wait_ge(oT_copied, 2)
            sp.dma_start(oT_dram, oT_out[:, :, :, :].rearrange("p k c m -> p (k c m)")).then_inc(oT_stored, 16)
            for t in range(NT):
                sp.wait_ge(x1_ready, t + 1)
                sp.dma_start(x1_dram[t * P:t * P + rows[t], :], X[0:rows[t], t, :]).then_inc(x1_out, 16)
            sp.wait_ge(uv_full, 4 * NC * STEPS)
            sp.wait_ge(oT_stored, 16)
            sp.dma_start(o_T[:, :, :, :].rearrange("p k c m -> p (k c m)"), oT_dram).then_inc(o_in, 16)
            with nc.allow_non_contiguous_dma(reason="256 biases, one to a partition"):
                sp.dma_start(o1_bias[:, :], o1_b.rearrange("(c p) -> p c", p=P)).then_inc(o_in, 16)
            sp.dma_start(o2_bias[:, :], o2_b.rearrange("(o m) -> o m", o=1).to_broadcast([P, DIM])).then_inc(x1_in, 16)
            sp.dma_start(x1_back[:, 0:FT, :], x1_dram[0:FT * P, :].rearrange("(t p) d -> p t d", p=P)).then_inc(x1_in, 16)
            sp.dma_start(x1_back[0:LAST, FT, :], x1_dram[FT * P:N, :]).then_inc(x1_in, 16)
            n = 0
            for t in range(0, NT, 2):
                n += 1
                sp.wait_ge(result_ready, min(t + 2, NT))
                if t + 1 < FT:
                    sp.dma_start(out[t * P:(t + 2) * P, :].rearrange("(t p) d -> p t d", p=P),
                                 result[:, t:t + 2, :]).then_inc(result_out, 16)
                else:
                    sp.dma_start(out[t * P:t * P + rows[t], :], result[0:rows[t], t, :]).then_inc(result_out, 16)
                    if t + 1 < NT:
                        n += 1
                        sp.dma_start(out[FT * P:N, :], result[0:LAST, FT, :]).then_inc(result_out, 16)
            sp.wait_ge(result_out, 16 * n)
            sp.wait_ge(x1_out, 16 * NT)

        @block.gpsimd
        def _(pool):
            pool.memset(ident, 0.0).then_inc(pool_done, 1)
            pool.wait_ge(pool_done, 1)
            pool.affine_select(out=ident_r[:, :], in_=ident, compare_op=ALU.not_equal, fill=1.0,
                               base=0, pattern=[[-1, P]], channel_multiplier=1).then_inc(ident_ready, 1)
            pool.memset(f32(ones[:, :]), 1.0).then_inc(ident_ready, 1)
            pool.wait_ge(gate_in[H], 16)
            for t in range(NT):
                pool.dma_start(A_rows[0:rows[t], t, :], adj[t * P:t * P + rows[t], :]).then_inc(adj_in[t], 16)

        @block.scalar
        def _(act):
            act.wait_ge(ident_ready, 2)
            act.activation(warm[:, 0:1], f32(ones[:, 0:1]), ACT.Sqrt)

            def gate_blocks(g):
                for pair in range(3):
                    f = 3 * g + pair
                    act.wait_ge(wt_full, f + 1)
                    dst = gate_T if pair < 2 else W_f32
                    kk = 2 * pair if pair < 2 else 4
                    act.activation(dst[:, kk:kk + 2, g * DIM:(g + 1) * DIM],
                                   gp[:, f % 4, :].rearrange("p (k m) -> p k m", k=2), ACT.Copy).then_inc(wt_copied, 1)

            for c in range(NC):
                act.wait_ge(mean_ready, c + 1)
                for t in chunk_tiles[c]:
                    act.activation(centred[0:rows[t], t, :], X[0:rows[t], t, :], ACT.Relu,
                                   bias=neg_mean[0:rows[t], t:t + 1]).then_inc(centred_ready, 1)
                if c == LC:
                    act.wait_ge(var_ready, 1)
                    act.activation(std[:, :], mean_var[:, :, 1], ACT.Sqrt).then_inc(std_ready, 1)
                if c < LC:
                    gate_blocks(c)
            act.activation(warm[:, 1:2], f32(ones[:, 0:1]), ACT.Exp)

            def fused(f):
                act.wait_ge(fused_full, f + 1)
                if f < 4:
                    act.activation(W_f32[:, f, 0:BANK], uvp[:, f, :], ACT.Copy).then_inc(fused_copied, 1)
                else:
                    act.activation(W_f32[:, f - 4, BANK:G3], gp[:, f - 4, 0:G3 - BANK],
                                   ACT.Copy).then_inc(fused_copied, 1)

            def leaky_scores(t):
                if t == 1:
                    act.wait_ge(a_ready, 2)
                if t >= 2:
                    act.wait_ge(score_ready, t - 1)
                act.activation(leaky[t % 2][0:rows[t], :], b_row[0:rows[t], :], ACT.Identity,
                               bias=a_col[0:rows[t], t:t + 1]).then_inc(leaky_ready, 1)

            def scale_h(tiles):
                for t in tiles:
                    p = rows[t]
                    act.activation(h[0:p, t, :], centred[0:p, t, :], ACT.Identity,
                                   scale=rstd[0:p, t:t + 1]).then_inc(h_ready, 1)

            fused(0)
            fused(1)
            for q, tiles in enumerate(fills):
                n = min(N, (tiles[-1] + 1) * P) - tiles[0] * P
                act.wait_ge(b_full, q + 1)
                act.activation(b_row[:, tiles[0] * P:tiles[0] * P + n], b_banks[q][:, 0:n], ACT.Copy).then_inc(b_copied, 1)
            act.wait_ge(b_copied, NF)
            act.wait_ge(a_ready, 1)
            leaky_scores(0)
            gate_blocks(H)
            fused(2)
            scale_h(range(H_SPLIT))
            fused(3)
            for k in range(2):
                act.wait_ge(oT_full, k + 1)
                act.activation(oT_out[:, k, :, :], uvp[:, k, :].rearrange("p (c m) -> p c m", c=2),
                               ACT.Copy).then_inc(oT_copied, 1)

            def columns(t):
                p = rows[t]
                for q, tiles in enumerate(fills):
                    act.wait_ge(at_full, NF * t + q + 1)
                    full = [k for k in tiles if k < FT]
                    last = act.activation(A_cols[:, full[0]:full[-1] + 1, t * P:t * P + p],
                                          gp[:, q, 0:len(full) * P].rearrange("p (k i) -> p k i", i=P)[:, :, 0:p],
                                          ACT.Copy)
                    if FT in tiles:
                        last = act.activation(A_cols[0:LAST, FT, t * P:t * P + p],
                                              gp[0:LAST, q, (FT - tiles[0]) * P:(FT - tiles[0]) * P + p],
                                              ACT.Copy)
                    last.then_inc(at_copied, 1)

            def probabilities(t):
                p = rows[t]
                act.wait_ge(score_ready, t + 1)
                act.activation(scores[0:p, t % 2, :], scores[0:p, t % 2, :], ACT.Exp,
                               bias=neg_max[0:p, t:t + 1],
                               accum_out=row_sum[0:p, t:t + 1]).then_inc(prob_ready, 1)

            def add_up_rows(t):
                p = rows[t]
                if t == 0:
                    act.wait_ge(h_ready, H_SPLIT)
                    act.wait_ge(late_h_ready, 1)
                else:
                    act.wait_ge(row_summed, t // 2)
                act.activation(row_copy[0:p, :], f32(A_rows[0:p, t, :]), ACT.Copy,
                               accum_out=degree_col[0:p, t:t + 1]).then_inc(row_summed, 1)

            assert NT % 2
            probabilities(0)
            leaky_scores(1)
            for t in range(NT):
                p = rows[t]
                if t >= 2:
                    act.wait_ge(att_full, t - 1)
                for q, tiles in enumerate(fills):
                    act.wait_ge(pt_full, NF * t + q + 1)
                    full = [k for k in tiles if k < FT]
                    last = act.activation(PT[:, t % 2, full[0]:full[-1] + 1, 0:p],
                                          uvp[:, q, 0:len(full) * P].rearrange("p (k i) -> p k i", i=P)[:, :, 0:p],
                                          ACT.Copy)
                    if FT in tiles:
                        last = act.activation(PT[0:LAST, t % 2, FT, 0:p],
                                              uvp[0:LAST, q, (FT - tiles[0]) * P:(FT - tiles[0]) * P + p],
                                              ACT.Copy)
                    last.then_inc(pt_copied, 1)
                if t == 0:
                    for f in range(4, 8):
                        fused(f)
                else:
                    if t == 1:
                        act.wait_ge(beta_ready, 12)
                    columns(t - 1)
                if t + 2 < NT:
                    leaky_scores(t + 2)
                if t + 1 < NT:
                    probabilities(t + 1)
                if t % 2 and t >= 3:
                    add_up_rows(t - 3)
            add_up_rows(NT - 3)
            add_up_rows(NT - 1)
            act.wait_ge(row_summed, 1)
            act.activation(warm[:, 0:1], f32(ones[:, 0:1]), ACT.Sqrt)
            columns(NT - 1)
            act.wait_ge(var_ready, 2)
            act.activation(std[:, :], mean_var[:, :, 1], ACT.Sqrt).then_inc(std_ready, 1)
            act.wait_ge(pt_full, NF * NT)
            act.wait_ge(score_ready, NT)
            for g in range(3):
                act.activation(W_hi[:, :, g * DIM:(g + 1) * DIM], W_f32[:, :, g * DIM:(g + 1) * DIM],
                               ACT.Copy).then_inc(w_hi_ready, 1)
            for c, (c0, n) in enumerate(chunks):
                act.wait_ge(degree_full, c + 1)
                act.activation(DEG[:, 1, c0:c0 + n], uvp[:, c, 0:n], ACT.Copy).then_inc(degree_ready, 1)
            act.wait_ge(oT_stored, 16)
            for f in range(2 * NC):
                c, m = divmod(f, 2)
                c0, n = chunks[c]
                bank = ln2_banks[f][:, 0:n]
                act.wait_ge(ln2_T_full, f + 1)
                act.activation(ST[:, m, c0:c0 + n], bank, ACT.Relu).then_inc(st_ready, 1)
            act.wait_ge(w_ready, 3)
            act.wait_ge(degree_full, 2 * NC)
            act.wait_ge(x1_out, 16 * NT)
            for c, (c0, n) in enumerate(chunks):
                act.activation(DEG[:, 0, c0:c0 + n], gp[:, c, 0:n], ACT.Copy).then_inc(degree_ready, 1)

            act.wait_ge(gate_b_in, 48)
            with act.Fori(0, STEPS) as step:
                def state_hi(k, bank, t0, count, p):
                    act.wait_ge(t_full, step * 6 + k + 1)
                    act.activation(S_hi[0:p, t0:t0 + count, :],
                                   bank[0:p, 0:count * DIM].rearrange("p (t d) -> p t d", d=DIM),
                                   ACT.Copy).then_inc(t_hi, 1)

                state_hi(0, gp[:, 2, :], late_tiles[0], len(late_tiles) - 1, P)
                state_hi(1, gp[:, 3, :], FT, 1, LAST)
                for c, (c0, n) in enumerate(chunks):
                    for b in range(4):
                        act.wait_ge(uv_full, step * 12 + 4 * c + b + 1)
                        act.activation(UV_hi[:, b, 0:n], uvp[:, b, 0:n], ACT.Copy).then_inc(uv_hi, 1)
                    for m in range(2):
                        act.wait_ge(r_sum, step * 6 + 2 * c + m + 1)
                        act.activation(gp[:, m, 0:n], gp[:, m, 0:n], ACT.Sigmoid,
                                       bias=gate_b[:, 2 * R + m:2 * R + m + 1]).then_inc(r_act, 1)
                    if c == LC:
                        for k in range(4):
                            state_hi(2 + k, uvp[:, k, :], 2 * k, 2, P)
                    for m in range(2):
                        act.wait_ge(z_sum, step * 6 + 2 * c + m + 1)
                        act.activation(gp[:, 2 + m, 0:n], gp[:, 2 + m, 0:n], ACT.Sigmoid,
                                       bias=gate_b[:, 2 * Z + m:2 * Z + m + 1]).then_inc(z_act, 1)
                    for m in range(2):
                        act.wait_ge(h_sum, step * 6 + 2 * c + m + 1)
                        act.activation(gp[:, m, 0:n], gp[:, m, 0:n], ACT.Tanh,
                                       bias=gate_b[:, 2 * H + m:2 * H + m + 1]).then_inc(h_act, 1)

            act.wait_ge(o_in, 32)
            for f in range(2 * NC):
                c, m = divmod(f, 2)
                c0, n = chunks[c]
                act.wait_ge(y_full, f + 1)
                act.activation(YT[:, m, c0:c0 + n], y_banks[f][:, 0:n], ACT.Tanh,
                               bias=o1_bias[:, m:m + 1]).then_inc(y_ready, 1)

        @block.vector
        def _(dve):
            chain = [0]

            def then(instruction):
                chain[0] += 1
                instruction.then_inc(dve_done, 1)
                dve.wait_ge(dve_done, chain[0])

            def statistics(tiles):
                for t in tiles:
                    last = dve.bn_stats(stats[0:rows[t], t, :], X[0:rows[t], t, :])
                then(last)
                for t in tiles:
                    last = dve.bn_aggr(mean_var[0:rows[t], t, :], stats[0:rows[t], t, :])
                return last

            def deviation():
                dve.tensor_scalar(mean_var[:, :, 1], mean_var[:, :, 1], EPS, None, ALU.add).then_inc(var_ready, 1)

            def reciprocal_deviation(turn):
                dve.wait_ge(std_ready, turn)
                then(dve.reciprocal(rstd[:, :], std[:, :]))
                then(dve.tensor_tensor(newton[:, :], rstd[:, :], rstd[:, :], ALU.mult))
                then(dve.tensor_tensor(newton[:, :], newton[:, :], mean_var[:, :, 1], ALU.mult))
                then(dve.tensor_scalar(newton[:, :], newton[:, :], -0.5, 1.5, ALU.mult, ALU.add))
                then(dve.tensor_tensor(rstd[:, :], rstd[:, :], newton[:, :], ALU.mult))

            def apply_a(half, col, t):
                p = rows[t]
                return dve.tensor_tensor_reduce(product[0:p, t, :], centred[0:p, t, :], a_bc[0:p, half, :], 1.0, 0.0,
                                                ALU.mult, ALU.add, col[0:p, t:t + 1])

            def normalise(t):
                p = rows[t]
                return dve.tensor_scalar(h[0:p, t, :], X[0:p, t, :], mean_var[0:p, t, 0:1], rstd[0:p, t:t + 1],
                                         ALU.subtract, ALU.mult)

            def penalty(t):
                p = rows[t]
                s = scores[0:p, t % 2, :]
                dve.wait_ge(adj_in[t], 16)
                if t >= 2:
                    dve.wait_ge(pt_full, NF * (t - 1))
                then(dve.tensor_scalar(s, f32(A_rows[0:p, t, :]), 0.0, NEG_BIG, ALU.is_le, ALU.mult))

            def score(t):
                p = rows[t]
                s = scores[0:p, t % 2, :]
                dve.wait_ge(leaky_ready, t + 1)
                then(dve.scalar_tensor_tensor(leaky[t % 2][0:p, :], leaky[t % 2][0:p, :], 0.01, leaky[t % 2][0:p, :],
                                              ALU.mult, ALU.max))
                then(dve.tensor_tensor_reduce(s, leaky[t % 2][0:p, :], s, 1.0, -3.0e38,
                                              ALU.subtract, ALU.max, row_max[0:p, t:t + 1]))
                dve.tensor_scalar(neg_max[0:p, t:t + 1], row_max[0:p, t:t + 1], -1.0, None,
                                  ALU.mult).then_inc(score_ready, 1)

            def residual(t):
                p = rows[t]
                bank = uvp[0:p, 3, 0:DIM] if t % 2 == 0 else gp[0:p, 3, 0:DIM]
                dve.wait_ge(prob_ready, t + 1)
                then(dve.reciprocal(inv_sum[0:p, t:t + 1], row_sum[0:p, t:t + 1]))
                dve.wait_ge(att_full, t + 1)
                last = dve.scalar_tensor_tensor(X[0:p, t, :], bank, inv_sum[0:p, t:t + 1], X[0:p, t, :],
                                                ALU.mult, ALU.add)
                last.then_inc(x1_ready, 1)
                dve.wait_ge(x1_ready, t + 1)
                return statistics([t])

            dve.memset(a_col[:, :], 0.0)
            dve.memset(b_col[:, :], 0.0)
            then(dve.memset(mean_var[:, :, :], 1.0))

            def apply_b(c):
                for t in chunk_tiles[c]:
                    dve.wait_ge(centred_ready, t + 1)
                    last = apply_a(1, b_col, t)
                return last

            def bias_of_gate(g):
                dve.wait_ge(gate_in[g], 16)
                dve.wait_ge(bias_in, 32)
                for k in range(2):
                    for m in range(2):
                        i = 2 * g + m
                        dve.tensor_tensor_reduce(bias_product[:, 6 * k + i, :], gate_nat[:, g, m, k * DIM:(k + 1) * DIM],
                                                 msg_bias[:, k, :], 1.0, 0.0, ALU.mult, ALU.add,
                                                 beta[:, k, i:i + 1]).then_inc(beta_ready, 1)

            dve.wait_ge(a_in, 16)
            for c, tiles in enumerate(chunk_tiles):
                dve.wait_ge(x_in[c], 32 if c == LC else 16)
                then(statistics(tiles))
                dve.tensor_scalar(neg_mean[:, tiles[0]:tiles[-1] + 1], mean_var[:, tiles[0]:tiles[-1] + 1, 0], -1.0,
                                  None, ALU.mult).then_inc(mean_ready, 1)
                if c == LC:
                    deviation()
                if c == 1:
                    bias_of_gate(Z)
                if c >= 1:
                    apply_b(c - 1)
            then(apply_b(LC))
            reciprocal_deviation(1)
            dve.tensor_tensor(b_col[:, :], b_col[:, :], rstd[:, :], ALU.mult).then_inc(b_ready, 1)
            dve.wait_ge(b_ready, 1)
            then(apply_a(0, a_col, 0))
            dve.tensor_tensor(a_col[:, 0:1], a_col[:, 0:1], rstd[:, 0:1], ALU.mult).then_inc(a_ready, 1)
            for t in range(1, NT):
                last = apply_a(0, a_col, t)
            then(last)
            dve.tensor_tensor(a_col[:, 1:NT], a_col[:, 1:NT], rstd[:, 1:NT], ALU.mult).then_inc(a_ready, 1)
            penalty(0)
            score(0)
            for t in range(H_SPLIT, NT):
                p = rows[t]
                last = dve.tensor_scalar(h[0:p, t, :], centred[0:p, t, :], rstd[0:p, t:t + 1], None, ALU.mult)
            last.then_inc(late_h_ready, 1)
            penalty(1)
            score(1)
            bias_of_gate(R)
            bias_of_gate(H)

            for t in range(NT):
                p = rows[t]
                if 1 <= t < NT - 1:
                    penalty(t + 1)
                    score(t + 1)
                if t >= 1:
                    residual(t - 1)
                if t >= 2 and t % 2 == 0:
                    dve.reduce_sum(degree_col[:, t - 1:t], f32(A_rows[:, t - 1, :]),
                                   mybir.AxisListType.X).then_inc(row_summed_odd, 1)
            then(residual(NT - 1))
            deviation()
            reciprocal_deviation(2)
            dve.wait_ge(att_full, NT)
            for t in range(NT):
                normalise(t).then_inc(ln2_ready, 1)
            early = len(early_tiles)
            dve.wait_ge(ln2_ready, early)
            then(dve.tensor_scalar(S_hi[:, 0:early, :], h[:, 0:early, :], 0.0, None, ALU.max))
            dve.wait_ge(ln2_T_full, 2 * LC)
            dve.scalar_tensor_tensor(S_lo[:, 0:early, :], h[:, 0:early, :], 0.0, f32(S_hi[:, 0:early, :]),
                                     ALU.max, ALU.subtract).then_inc(t_ready, 1)
            for g in range(3):
                cols = slice(g * DIM, (g + 1) * DIM)
                dve.wait_ge(w_hi_ready, g + 1)
                dve.tensor_tensor(W_lo[:, :, cols], W_f32[:, :, cols], f32(W_hi[:, :, cols]),
                                  ALU.subtract).then_inc(w_ready, 1)
            dve.wait_ge(w_ready, 3)
            dve.wait_ge(x1_out, 16 * NT)
            dve.wait_ge(st_ready, 2 * NC)
            dve.memset(tmp[0:1, 0:2], 0.0).then_inc(updated, 1)

            with dve.Fori(0, STEPS) as step:
                links = [0]
                per_step = 13 * NC

                def link(instruction):
                    links[0] += 1
                    instruction.then_inc(loop_done, 1)
                    dve.wait_ge(loop_done, step * per_step + links[0])

                def split_chunk(c):
                    c0, n = chunks[c]
                    link(dve.tensor_copy(SC_hi[:, :, 0:n], ST[:, :, c0:c0 + n]))
                    dve.tensor_tensor(SC_lo[:, :, 0:n], ST[:, :, c0:c0 + n], f32(SC_hi[:, :, 0:n]),
                                      ALU.subtract).then_inc(sc_ready, 1)

                def state_lo(k, bank, t0, count, p):
                    dve.wait_ge(t_hi, step * 6 + k + 1)
                    dve.tensor_tensor(S_lo[0:p, t0:t0 + count, :],
                                      bank[0:p, 0:count * DIM].rearrange("p (t d) -> p t d", d=DIM),
                                      f32(S_hi[0:p, t0:t0 + count, :]), ALU.subtract).then_inc(t_ready, 1)

                def add_degrees(full, sums, g, b0, c):
                    c0, n = chunks[c]
                    for m in range(2):
                        bank = gp[:, b0 + m, 0:n]
                        dve.wait_ge(full, step * 6 + 2 * c + m + 1)
                        if c == 0 and g == R and m == 0:
                            dve.wait_ge(degree_ready, 2 * NC)
                        link(dve.scalar_tensor_tensor(bank, DEG[:, 0, c0:c0 + n], beta[:, 0, 2 * g + m:2 * g + m + 1],
                                                      bank, ALU.mult, ALU.add))
                        dve.scalar_tensor_tensor(bank, DEG[:, 1, c0:c0 + n], beta[:, 1, 2 * g + m:2 * g + m + 1],
                                                 bank, ALU.mult, ALU.add).then_inc(sums, 1)

                split_chunk(0)
                state_lo(0, gp[:, 2, :], late_tiles[0], len(late_tiles) - 1, P)
                state_lo(1, gp[:, 3, :], FT, 1, LAST)
                for c, (c0, n) in enumerate(chunks):
                    for b in range(4):
                        dve.wait_ge(uv_hi, step * 12 + 4 * c + b + 1)
                        dve.tensor_tensor(UV_lo[:, b, 0:n], uvp[:, b, 0:n], f32(UV_hi[:, b, 0:n]),
                                          ALU.subtract).then_inc(uv_ready, 1)
                    add_degrees(r_full, r_sum, R, 0, c)
                    for m in range(2):
                        dve.wait_ge(r_act, step * 6 + 2 * c + m + 1)
                        if m == 1:
                            dve.wait_ge(rs_ready, step * 6 + 2 * c + 1)
                        ins = dve.tensor_tensor(tmp[:, 0:n], gp[:, m, 0:n], ST[:, m, c0:c0 + n], ALU.mult)
                        ins.then_inc(r_used, 1)
                        dve.wait_ge(r_used, step * 6 + 2 * c + m + 1)
                        link(dve.tensor_copy(SC_hi[:, m, 0:n], tmp[:, 0:n]))
                        dve.tensor_tensor(SC_lo[:, m, 0:n], tmp[:, 0:n], f32(SC_hi[:, m, 0:n]),
                                          ALU.subtract).then_inc(rs_ready, 1)
                    if c == LC:
                        for k in range(4):
                            state_lo(2 + k, uvp[:, k, :], 2 * k, 2, P)
                    add_degrees(z_full, z_sum, Z, 2, c)
                    add_degrees(h_full, h_sum, H, 0, c)
                    for m in range(2):
                        dve.wait_ge(h_act, step * 6 + 2 * c + m + 1)
                        if m == 0:
                            dve.wait_ge(rs_ready, step * 6 + 2 * c + 2)
                        else:
                            dve.wait_ge(updated, step * 6 + 2 * c + 2)
                        link(dve.tensor_tensor(tmp[:, 0:n], gp[:, m, 0:n], ST[:, m, c0:c0 + n], ALU.subtract))
                        dve.wait_ge(z_act, step * 6 + 2 * c + m + 1)
                        link(dve.tensor_tensor(tmp[:, 0:n], gp[:, 2 + m, 0:n], tmp[:, 0:n], ALU.mult))
                        dve.tensor_tensor(ST[:, m, c0:c0 + n], ST[:, m, c0:c0 + n], tmp[:, 0:n],
                                          ALU.add).then_inc(updated, 1)
                    dve.wait_ge(updated, step * 6 + 2 * c + 3)
                    if c < LC:
                        split_chunk(c + 1)
                assert links[0] == per_step

            dve.wait_ge(x1_in, 48)
            for t in range(NT):
                p = rows[t]
                last = dve.tensor_tensor(x1_back[0:p, t, :], x1_back[0:p, t, :], o2_bias[0:p, :], ALU.add)
            last.then_inc(x1b_ready, 1)
            dve.wait_ge(x1b_ready, 1)
            for t in range(NT):
                p = rows[t]
                dve.wait_ge(r_out_full, t + 1)
                dve.tensor_tensor(result[0:p, t, :], out_banks[t % 4][0:p, 0:DIM], x1_back[0:p, t, :],
                                  ALU.add).then_inc(result_ready, 1)

        @block.tensor
        def _(pe):
            pe.wait_ge(ident_ready, 2)
            def gate_blocks(g):
                pe.wait_ge(gate_in[g], 16)
                for pair in range(3):
                    f = 3 * g + pair
                    if f >= 4:
                        pe.wait_ge(wt_copied, f - 3)
                    for kk in range(2):
                        for m in range(2):
                            k0 = (2 * pair + kk) * P
                            last = pe.transpose(gp[:, f % 4, kk * DIM + m * P:kk * DIM + (m + 1) * P],
                                                gate_nat[:, g, m, k0:k0 + P], ident)
                    last.then_inc(wt_full, 1)

            def fuse(kt, bank, c0, n):
                k, half = divmod(kt, 2)
                for tt in range(2):
                    last = pe.matmul(bank[:, kt, 0:n], msg_nat[:, k, tt, half * P:(half + 1) * P],
                                     gate_T[:, 2 * k + tt, c0:c0 + n], start=(tt == 0), stop=(tt == 1))
                last.then_inc(fused_full, 1)

            assert (Z, R, H) == (0, 1, 2) and 2 * DIM == BANK
            gate_blocks(Z)
            gate_blocks(R)
            pe.wait_ge(msg_in, 32)
            pe.wait_ge(wt_copied, 6)
            fuse(0, uvp, 0, BANK)
            fuse(1, uvp, 0, BANK)
            pe.wait_ge(b_ready, 1)
            for q, tiles in enumerate(fills):
                for t in tiles:
                    p = rows[t]
                    last = pe.matmul(b_banks[q][:, (t - tiles[0]) * P:(t - tiles[0]) * P + p],
                                     b_col[0:p, t:t + 1].to_broadcast([p, P]), f32(ident_r[0:p, 0:p]),
                                     start=True, stop=True)
                last.then_inc(b_full, 1)
            gate_blocks(H)
            pe.wait_ge(b_copied, NF)
            fuse(2, uvp, 0, BANK)
            fuse(3, uvp, 0, BANK)
            pe.wait_ge(o_nat_in, 32)
            pe.wait_ge(fused_copied, 2)
            for k in range(2):
                for c in range(2):
                    for m in range(2):
                        last = pe.transpose(uvp[:, k, c * DIM + m * P:c * DIM + (m + 1) * P],
                                            o_nat[:, k, m, c * P:(c + 1) * P], ident)
                last.then_inc(oT_full, 1)
            pe.wait_ge(wt_copied, 9)
            for kt in range(4):
                fuse(kt, gp, BANK, G3 - BANK)

            def transpose_adjacency(t):
                p = rows[t]
                pe.wait_ge(adj_in[t], 16)
                for q, tiles in enumerate(fills):
                    if t >= 1:
                        pe.wait_ge(at_copied, NF * (t - 1) + q + 1)
                    else:
                        pe.wait_ge(fused_copied, 5 + q)
                    for k in tiles:
                        last = pe.transpose(gp[0:rows[k], q, (k - tiles[0]) * P:(k - tiles[0]) * P + p].bitcast(F32R),
                                            A_rows[0:p, t, k * P:k * P + rows[k]], ident_r[0:p, 0:p])
                    last.then_inc(at_full, 1)

            pe.wait_ge(fused_copied, 4)
            pe.wait_ge(oT_copied, 2)
            for t in range(NT):
                p = rows[t]
                pe.wait_ge(prob_ready, t + 1)
                for q, tiles in enumerate(fills):
                    if t >= 1:
                        pe.wait_ge(pt_copied, NF * (t - 1) + q + 1)
                    for k in tiles:
                        last = pe.transpose(uvp[0:rows[k], q, (k - tiles[0]) * P:(k - tiles[0]) * P + p],
                                            scores[0:p, t % 2, k * P:k * P + rows[k]], f32(ident_r[0:p, 0:p]))
                    last.then_inc(pt_full, 1)
                if t >= 1:
                    transpose_adjacency(t - 1)
                if t >= 2:
                    pe.wait_ge(x1_ready, t - 1)
                elif t == 1:
                    pe.wait_ge(fused_copied, 8)
                bank = uvp[0:p, 3, 0:DIM] if t % 2 == 0 else gp[0:p, 3, 0:DIM]
                for k in range(NT):
                    if k % TPC == 0:
                        pe.wait_ge(pt_copied, NF * t + k // TPC + 1)
                    if t == 0 and k < H_SPLIT:
                        pe.wait_ge(h_ready, k + 1)
                    elif t == 0:
                        pe.wait_ge(late_h_ready, 1)
                    last = pe.matmul(bank, PT[0:rows[k], t % 2, k, 0:p], h[0:rows[k], k, :],
                                     start=(k == 0), stop=(k == NT - 1))
                last.then_inc(att_full, 1)
            transpose_adjacency(NT - 1)
            for c, (c0, n) in enumerate(chunks):
                pe.wait_ge(pt_copied, NF * (NT - 1) + c + 1)
                for t in range(NT):
                    last = pe.matmul(uvp[:, c, 0:n], ones[0:rows[t], :], A_rows[0:rows[t], t, c0:c0 + n],
                                     start=(t == 0), stop=(t == NT - 1))
                last.then_inc(degree_full, 1)
            for f in range(2 * NC):
                c, m = divmod(f, 2)
                bank = ln2_banks[f]
                if f < NF:
                    pe.wait_ge(at_copied, NF * (NT - 1) + f + 1)
                elif f < 5:
                    pe.wait_ge(x1_ready, NT)
                else:
                    pe.wait_ge(degree_ready, 1)
                for t in chunk_tiles[c]:
                    p = rows[t]
                    i0 = t * P - chunks[c][0]
                    pe.wait_ge(ln2_ready, t + 1)
                    last = pe.transpose(bank[:, i0:i0 + p], h[0:p, t, m * P:(m + 1) * P], f32(ident_r[0:p, 0:p]))
                last.then_inc(ln2_T_full, 1)
            pe.wait_ge(row_summed, -(-NT // 2))
            pe.wait_ge(row_summed_odd, NT // 2)
            for q, tiles in enumerate(fills):
                pe.wait_ge(st_ready, q + 1)
                for t in tiles:
                    p = rows[t]
                    last = pe.matmul(gp[:, q, (t - tiles[0]) * P:(t - tiles[0]) * P + p],
                                     degree_col[0:p, t:t + 1].to_broadcast([p, P]), f32(ident_r[0:p, 0:p]),
                                     start=True, stop=True)
                last.then_inc(degree_full, 1)
            pe.wait_ge(st_ready, 2 * NC)

            with pe.Fori(0, STEPS) as step:
                def propagate(b, c, tiles, first, final):
                    c0, n = chunks[c]
                    m = b % 2
                    A = A_cols if b < 2 else A_rows
                    for t in tiles:
                        p = rows[t]
                        for part in (S_hi, S_lo):
                            ins = pe.matmul(uvp[:, b, 0:n], part[0:p, t, m * P:(m + 1) * P], A[0:p, t, c0:c0 + n],
                                            start=(first and t == tiles[0] and part is S_hi),
                                            stop=(final and t == tiles[-1] and part is S_lo))
                    if final:
                        ins.then_inc(uv_full, 1)

                def transpose_state(bank, tiles, column=0):
                    for i, t in enumerate(tiles):
                        p = rows[t]
                        for m in range(2):
                            ins = pe.transpose(bank[0:p, i * DIM + m * P:i * DIM + (m + 1) * P],
                                               ST[:, m, t * P:t * P + p], ident)
                    ins.then_inc(t_full, 1)

                def gate(bank, n, g, m, operands, first, final):
                    cols = slice(g * DIM + m * P, g * DIM + (m + 1) * P)
                    for i, (kt, hi, lo) in enumerate(operands):
                        for j, (w, v) in enumerate(((W_hi, hi), (W_hi, lo), (W_lo, hi))):
                            ins = pe.matmul(bank, w[:, kt, cols], v, start=(first and i == 0 and j == 0),
                                            stop=(final and i == len(operands) - 1 and j == 2))
                    return ins

                pe.wait_ge(t_ready, step * 6 + 1)
                for b in range(3):
                    propagate(b, 0, early_tiles, True, False)
                pe.wait_ge(updated, step * 6 + 1)
                pe.wait_ge(degree_ready, 2 * NC)
                transpose_state(gp[:, 2, :], late_tiles[:-1])
                transpose_state(gp[:, 3, :], late_tiles[-1:])
                propagate(3, 0, early_tiles, True, False)
                pe.wait_ge(t_ready, step * 6 + 3)
                for c, (c0, n) in enumerate(chunks):
                    for b in range(4):
                        if c == 0:
                            propagate(b, 0, late_tiles, False, True)
                        else:
                            pe.wait_ge(uv_ready, step * 12 + 4 * (c - 1) + b + 1)
                            propagate(b, c, list(range(NT)), True, True)
                    state = [(4 + k, SC_hi[:, k, 0:n], SC_lo[:, k, 0:n]) for k in range(2)]
                    message = [(k, UV_hi[:, k, 0:n], UV_lo[:, k, 0:n]) for k in range(4)]
                    pe.wait_ge(sc_ready, step * 3 + c + 1)
                    if c == 0:
                        pe.wait_ge(w_ready, 3)
                    if c > 0:
                        pe.wait_ge(updated, step * 6 + 2 * c + 1)
                    for g, b0 in ((R, 0), (Z, 2)):
                        for m in range(2):
                            gate(gp[:, b0 + m, 0:n], n, g, m, state, True, False)
                    pe.wait_ge(uv_ready, step * 12 + 4 * (c + 1))
                    for m in range(2):
                        gate(gp[:, m, 0:n], n, R, m, message, False, True).then_inc(r_full, 1)
                    if c == LC:
                        for k in range(4):
                            transpose_state(uvp[:, k, :], [2 * k, 2 * k + 1])
                    for m in range(2):
                        gate(gp[:, 2 + m, 0:n], n, Z, m, message, False, True).then_inc(z_full, 1)
                    for m in range(2):
                        pe.wait_ge(r_used, step * 6 + 2 * c + m + 1)
                        gate(gp[:, m, 0:n], n, H, m, message, True, False)
                    pe.wait_ge(rs_ready, step * 6 + 2 * c + 2)
                    for m in range(2):
                        gate(gp[:, m, 0:n], n, H, m, state, False, True).then_inc(h_full, 1)

            pe.wait_ge(o_in, 32)
            pe.wait_ge(t_ready, 6 * STEPS + 1)
            for f in range(2 * NC):
                c, m = divmod(f, 2)
                c0, n = chunks[c]
                pe.wait_ge(updated, 6 * (STEPS - 1) + 2 * c + 3)
                for k in range(2):
                    last = pe.matmul(y_banks[f][:, 0:n], o_T[:, 0, k, m * P:(m + 1) * P], ST[:, k, c0:c0 + n],
                                     start=(k == 0), stop=(k == 1))
                last.then_inc(y_full, 1)
            for t in range(NT):
                p = rows[t]
                pe.wait_ge(y_ready, 2 * (t * P // BANK) + 2)
                if t >= 4:
                    pe.wait_ge(result_ready, t - 3)
                for k in range(2):
                    last = pe.matmul(out_banks[t % 4][0:p, 0:DIM], YT[:, k, t * P:t * P + p], o_T[:, 1, k, :],
                                     start=(k == 0), stop=(k == 1))
                last.then_inc(r_out_full, 1)


_INS = ['x', 'adj', 'L0_gnn_a', 'L1_gnn_in_W', 'L1_gnn_in_b', 'L1_gnn_out_W', 'L1_gnn_out_b', 'L1_gnn_r_W',
        'L1_gnn_r_b', 'L1_gnn_z_W', 'L1_gnn_z_b', 'L1_gnn_h_W', 'L1_gnn_h_b', 'L1_gnn_o1_W', 'L1_gnn_o1_b',
        'L1_gnn_o2_W', 'L1_gnn_o2_b']


def kernel(**inputs):
    import numpy as _np
    import concourse.bacc as _bacc
    from concourse import mybir as _mybir
    from concourse.bass_utils import run_bass_kernel_spmd as _run

    nc = _bacc.Bacc("TRN2", target_bir_lowering=False, num_devices=1, dynamic_dma_scratch_size=1024)
    arrays, args = {}, []
    for name in _INS:
        a = _np.ascontiguousarray(inputs[name])
        arrays[f"in_{name}_dram"] = a
        args.append(nc.dram_tensor(f"in_{name}_dram", a.shape, _mybir.dt.from_np(a.dtype), kind="ExternalInput").ap())
    args.append(nc.dram_tensor("out_0_dram", inputs['x'].shape, _mybir.dt.float32, kind="ExternalOutput").ap())
    gat_ggnn_kernel(nc, *args)
    r = _run(nc, [arrays], core_ids=[0])
    return r.results[0]["out_0_dram"]
```
